# Optimizing a Trainium2 kernel written in Bass

```python
import numpy as np
import jax
import jax.numpy as jnp

def _softmax(x, axis=-1):
    return jax.nn.softmax(x, axis=axis)

def _gelu(x):
    return jax.nn.gelu(x, approximate=True)

def _silu(x):
    return jax.nn.silu(x)

def _sigmoid(x):
    return jax.nn.sigmoid(x)

def _layernorm(x, axis=-1, eps=1e-05):
    m = jnp.mean(x, axis=axis, keepdims=True)
    v = jnp.var(x, axis=axis, keepdims=True)
    return (x - m) / jnp.sqrt(v + eps)

def _scatter_add(tgt, idx, src, axis=0):
    return tgt.at[idx].add(src)

def _segment_sum(src, seg, n):
    return jax.ops.segment_sum(src, seg, n)
kernel_name = 'mk_gnn_preln_d1_gnn_r32_5dee34'

def setup_inputs(seed: int=0):
    np.random.seed(seed)
    _w = jnp.asarray

    def _rec_inputs():
        import jax
        import jax.numpy as jnp
        _gk = jax.random.key(seed)
        x = -0.000364 + 1 * jax.random.normal(jax.random.fold_in(_gk, 1), (625, 768), jnp.float32)
        src = jax.random.randint(jax.random.fold_in(_gk, 2), (20000,), 0, 625, jnp.int32)
        dst = jax.random.randint(jax.random.fold_in(_gk, 3), (20000,), 0, 625, jnp.int32)
        _o = jnp.argsort(dst, stable=True)
        src = src[_o]
        dst = dst[_o]
        return (x, src, dst)
    x, src, dst = _rec_inputs()

    def _L0_gnn_setup():
        import jax, jax.numpy as jnp
        import numpy as np
        N, E, DIM, HEADS = (625, 10000, 768, 8)
        HD = DIM // HEADS
        EPS = 1e-05

        def layer_norm(x, w, b):
            mu = jnp.mean(x, axis=-1, keepdims=True)
            var = jnp.var(x, axis=-1, keepdims=True)
            return (x - mu) * jax.lax.rsqrt(var + EPS) * w + b

        def gatv2(x, src, dst, Ws, bs, Wd, bd, attn):
            H, D = attn.shape
            fs = (x @ Ws + bs).reshape(-1, H, D)
            fd = (x @ Wd + bd).reshape(-1, H, D)
            e = jax.nn.leaky_relu(fs[src] + fd[dst], 0.2)
            logits = jnp.einsum('ehd,hd->eh', e, attn)
            m = jax.ops.segment_max(logits, dst, num_segments=N)
            ex = jnp.exp(logits - m[dst])
            denom = jax.ops.segment_sum(ex, dst, num_segments=N)
            alpha = ex / denom[dst]
            out = jax.ops.segment_sum(alpha[:, :, None] * fs[src], dst, num_segments=N)
            return jax.nn.elu(out)
        key = jax.random.key(seed)
        ks = jax.random.split(key, 10)
        s = 1.0 / np.sqrt(DIM)
        return {'x': jax.random.normal(ks[0], (N, DIM), jnp.float32), 'src': jax.random.randint(ks[1], (E,), 0, N, jnp.int32), 'dst': jax.random.randint(ks[2], (E,), 0, N, jnp.int32), 'W1s': jax.random.normal(ks[3], (DIM, DIM), jnp.float32) * s, 'b1s': jnp.zeros((DIM,), jnp.float32), 'W1d': jax.random.normal(ks[4], (DIM, DIM), jnp.float32) * s, 'b1d': jnp.zeros((DIM,), jnp.float32), 'attn1': jax.random.normal(ks[5], (HEADS, HD), jnp.float32) * s, 'ln1_w': jnp.ones((DIM,), jnp.float32), 'ln1_b': jnp.zeros((DIM,), jnp.float32), 'Wos': jax.random.normal(ks[6], (DIM, DIM), jnp.float32) * s, 'bos': jnp.zeros((DIM,), jnp.float32), 'Wod': jax.random.normal(ks[7], (DIM, DIM), jnp.float32) * s, 'bod': jnp.zeros((DIM,), jnp.float32), 'attno': jax.random.normal(ks[8], (1, DIM), jnp.float32) * s, 'lno_w': jnp.ones((DIM,), jnp.float32), 'lno_b': jnp.zeros((DIM,), jnp.float32)}
    _L0_gnn_all = _L0_gnn_setup()
    _L0_gnn_in = {k: v for k, v in _L0_gnn_all.items() if k in ('W1s', 'b1s', 'W1d', 'b1d', 'attn1', 'ln1_w', 'ln1_b', 'Wos', 'bos', 'Wod', 'bod', 'attno', 'lno_w', 'lno_b')}
    del _L0_gnn_all
    return {'x': x, 'src': src, 'dst': dst, 'L0_gnn_W1s': _L0_gnn_in['W1s'], 'L0_gnn_b1s': _L0_gnn_in['b1s'], 'L0_gnn_W1d': _L0_gnn_in['W1d'], 'L0_gnn_b1d': _L0_gnn_in['b1d'], 'L0_gnn_attn1': _L0_gnn_in['attn1'], 'L0_gnn_ln1_w': _L0_gnn_in['ln1_w'], 'L0_gnn_ln1_b': _L0_gnn_in['ln1_b'], 'L0_gnn_Wos': _L0_gnn_in['Wos'], 'L0_gnn_bos': _L0_gnn_in['bos'], 'L0_gnn_Wod': _L0_gnn_in['Wod'], 'L0_gnn_bod': _L0_gnn_in['bod'], 'L0_gnn_attno': _L0_gnn_in['attno'], 'L0_gnn_lno_w': _L0_gnn_in['lno_w'], 'L0_gnn_lno_b': _L0_gnn_in['lno_b']}

def reference(x, src, dst, L0_gnn_W1s, L0_gnn_b1s, L0_gnn_W1d, L0_gnn_b1d, L0_gnn_attn1, L0_gnn_ln1_w, L0_gnn_ln1_b, L0_gnn_Wos, L0_gnn_bos, L0_gnn_Wod, L0_gnn_bod, L0_gnn_attno, L0_gnn_lno_w, L0_gnn_lno_b):
    import jax
    import jax.numpy as jnp

    def _L0_gnn_ref(x, src, dst, W1s, b1s, W1d, b1d, attn1, ln1_w, ln1_b, Wos, bos, Wod, bod, attno, lno_w, lno_b):
        import jax, jax.numpy as jnp
        import numpy as np
        N, E, DIM, HEADS = (625, 10000, 768, 8)
        HD = DIM // HEADS
        EPS = 1e-05

        def layer_norm(x, w, b):
            mu = jnp.mean(x, axis=-1, keepdims=True)
            var = jnp.var(x, axis=-1, keepdims=True)
            return (x - mu) * jax.lax.rsqrt(var + EPS) * w + b

        def gatv2(x, src, dst, Ws, bs, Wd, bd, attn):
            H, D = attn.shape
            fs = (x @ Ws + bs).reshape(-1, H, D)
            fd = (x @ Wd + bd).reshape(-1, H, D)
            e = jax.nn.leaky_relu(fs[src] + fd[dst], 0.2)
            logits = jnp.einsum('ehd,hd->eh', e, attn)
            m = jax.ops.segment_max(logits, dst, num_segments=N)
            ex = jnp.exp(logits - m[dst])
            denom = jax.ops.segment_sum(ex, dst, num_segments=N)
            alpha = ex / denom[dst]
            out = jax.ops.segment_sum(alpha[:, :, None] * fs[src], dst, num_segments=N)
            return jax.nn.elu(out)
        h = gatv2(x, src, dst, W1s, b1s, W1d, b1d, attn1).reshape(N, DIM)
        h = layer_norm(h + x, ln1_w, ln1_b)
        out = gatv2(h, src, dst, Wos, bos, Wod, bod, attno).reshape(N, DIM)
        return layer_norm(out, lno_w, lno_b)
    h = jnp.maximum(_layernorm(x, axis=-1), 0.0)
    x = x + _L0_gnn_ref(h, src, dst, L0_gnn_W1s, L0_gnn_b1s, L0_gnn_W1d, L0_gnn_b1d, L0_gnn_attn1, L0_gnn_ln1_w, L0_gnn_ln1_b, L0_gnn_Wos, L0_gnn_bos, L0_gnn_Wod, L0_gnn_bod, L0_gnn_attno, L0_gnn_lno_w, L0_gnn_lno_b)
    return x

_drawn_inputs = setup_inputs


def setup_inputs(seed=0):
    import zlib

    import numpy as np

    out = dict(_drawn_inputs(seed))
    spreads = {'L0_gnn_b1s': (0.0, 0.1),
     'L0_gnn_b1d': (0.0, 0.8),
     'L0_gnn_ln1_w': (1.0, 0.2),
     'L0_gnn_ln1_b': (0.0, 0.1),
     'L0_gnn_bos': (0.0, 0.1),
     'L0_gnn_bod': (0.0, 0.8),
     'L0_gnn_lno_w': (1.0, 0.2),
     'L0_gnn_lno_b': (0.0, 0.1)}
    factors = {'L0_gnn_W1d': 8.0, 'L0_gnn_attn1': 3.512}
    for name, (base, spread) in spreads.items():
        noise = np.random.default_rng([zlib.crc32(name.encode()), seed]).standard_normal(out[name].shape)
        drawn = base * np.exp(spread * noise) if base else spread * noise
        out[name] = jnp.asarray(drawn.astype(out[name].dtype))
    for name, factor in factors.items():
        out[name] = (out[name] * factor).astype(out[name].dtype)
    return out
```

```python
import concourse.bass as bass
from concourse import mybir
from contextlib import ExitStack


P = 128
N = 625
NB = 5
NP = NB * P
D = 768
H = 8
HD = D // H
KC = D // P
E = 20000
TE = 125
TU = E // TE
QJ = 4
Q = TU // QJ
LO = 32
UN = 6
T = 162
assert T * P >= E + NB * (P - 1) and T % UN == 0
UK = T // UN
CH = 16
TC = 11
TP = CH * TC
L = TC * P
FW = D + H
EPS = 1e-5
SLOPE = 0.2
BIG = 1e30
HB = 256
DEN = NB * D
CHUNK = 4
CE = E // CHUNK
CTU = TU // CHUNK
UP = 4
QG = 8

f32 = mybir.dt.float32
bf16 = mybir.dt.bfloat16
f16 = mybir.dt.float16
i32 = mybir.dt.int32
ALU = mybir.AluOpType
ACT = mybir.ActivationFunctionType
AX = mybir.AxisListType


PROJ = [("T", 0), ("T", 1), ("F", 0), ("T", 2), ("F", 1), ("T", 3), ("F", 2), ("T", 4),
        ("F", 3), ("F", 4), ("D", 0), ("D", 1), ("D", 2), ("D", 3), ("D", 4)]


def live(s, back, n=T):
    return not isinstance(s, int) or 0 <= s - back < n


def tiles(eng, body, lag=0, n=T, un=UN):
    for s in range(un):
        body(s, s, 0)
    with eng.Fori(1, n // un) as k:
        for j in range(un):
            body(k * un + j, j, k)
    for s in range(n, n + lag):
        body(s, s % un, s // un)



def gnn_program(nc, x, src, dst, W1s, b1s, W1d, b1d, attn1, ln1_w, ln1_b,
                Wos, bos, Wod, bod, attno, lno_w, lno_b, out):
    ctx = ExitStack()
    with ctx:
        def sb(name, shape, dt):
            return ctx.enter_context(nc.sbuf_tensor(name, shape, dt))

        def sem(name):
            return ctx.enter_context(nc.semaphore(name))

        tables = [nc.dram_tensor(f"fs_table{l}", (NP, FW), f32, kind="Internal").ap() for l in range(2)]
        dl_rows = nc.dram_tensor("dl_rows", (T, P), bf16, kind="Internal").ap()

        R1 = sb("R1", [P, T * P // 2], f32)
        onehotT = R1[:, :].bitcast(bf16)
        dst_row = [R1[0:TE, c * CE:(c + 1) * CE].bitcast(i32) for c in range(2)]
        GW, ZW, YW = UN * FW, 3 * FW, 2 * D
        R2W = max(GW + ZW + YW + 2 * L, TU * LO + Q * TE + 2 * Q * LO)
        R2 = sb("R2", [P, R2W], f32)
        G = [R2[:, i * FW:(i + 1) * FW] for i in range(UN)]
        Z = [R2[:, GW + i * FW:GW + (i + 1) * FW] for i in range(3)]
        Y = [R2[:, GW + ZW + i * D:GW + ZW + (i + 1) * D] for i in range(2)]
        WG = [R2[:, GW + i * D:GW + (i + 1) * D] for i in range(3)]
        oh_agg = [R2[:, GW + 3 * D + i * P:GW + 3 * D + (i + 1) * P] for i in range(3)]
        reset_f = R2[:, R2W - 2 * L:R2W - L]
        reset_b = R2[:, R2W - L:R2W]
        LT, FWD, BWD = (R2[:, i * L:(i + 1) * L] for i in range(3))
        assert 3 * L <= GW
        evac = [R2[:, i * D:(i + 1) * D] for i in range(4)]
        lnw_row, lnb_row = (R2[:, GW + i * D:GW + (i + 1) * D] for i in range(2))
        OH = R2[0:TE, 0:TU * LO // 2].bitcast(bf16).rearrange("p (t l) -> p t l", l=LO)
        OL = R2[0:TE, TU * LO // 2:TU * LO].bitcast(bf16).rearrange("p (t l) -> p t l", l=LO)
        OHT = R2[:, TU * LO:TU * LO + Q * TE].rearrange("p (q e) -> p q e", e=TE)
        raw = R2[0:80, TU * LO:TU * LO + 4 * TE].bitcast(i32).rearrange("q (v p) -> q v p", p=TE)
        rawf = R2[0:80, TU * LO + 4 * TE:TU * LO + 8 * TE].rearrange("q (v p) -> q v p", p=TE)
        CT = R2[:, TU * LO + Q * TE:TU * LO + Q * TE + Q * LO]
        TAB = R2[:, TU * LO + Q * TE + Q * LO:TU * LO + Q * TE + 2 * Q * LO]
        sel = [R2[0:TE, i * QJ * QG * LO:(i + 1) * QJ * QG * LO] for i in range(2)]
        at = QJ * QG * LO
        perm_l = [R2[0:TE, at + i * P // 2:at + (i + 1) * P // 2].bitcast(f16) for i in range(UP)]
        at += UP * P // 2
        perm_r = [R2[0:TE, at + i * T:at + (i + 1) * T].bitcast(f16) for i in range(UP)]
        assert at + UP * T <= TU * LO // 2

        h0 = sb("h0", [P, NB, D], f32)
        R3 = sb("R3", [P, KC * NP], f32)
        hT = R3[:, :].rearrange("p (k n) -> p k n", k=KC)
        logits = R3[:, 0:TP * H]
        ulog = R3[:, TP * H:2 * TP * H]
        assert 2 * TP * H <= KC * NP
        Wm = sb("Wm", [P, KC, D], f32)
        bias = [sb(f"bias{i}", [P, D], f32) for i in range(2)]
        attn_row = sb("attn_row", [P, D], f32)
        FD = [sb(f"FD{i}", [P, NB * FW], bf16) for i in range(3)]
        ftile = [sb(f"ftile{i}", [P, FW], f32) for i in range(2)]
        utmp = sb("utmp", [P, D], f32)

        ident = sb("ident", [P, P], f32)
        identb = sb("identb", [P, P], bf16)
        diff = sb("diff", [P, P], f32)
        ltmask = sb("ltmask", [P, P], f32)
        shift_up = sb("shift_up", [P, P], f32)
        shift_dn = sb("shift_dn", [P, P], f32)
        iota_t = sb("iota_t", [P, T + UN], f32)
        iota_h = sb("iota_h", [P, T + UN], f16)
        iota_p = sb("iota_p", [P, 1], f32)
        zeros = sb("zeros", [P, 512], bf16)
        zerof = sb("zerof", [P, LO], f32)
        ones = sb("ones", [P, P], f32)
        ci = sb("ci", [P, 4, P], i32)
        pi = sb("pi", [P, 4], i32)
        pf = sb("pf", [P, 4], f32)
        M = sb("M", [P, 4, P], f32)
        Mhi, Mj, Mless, Msame = (M[:, i, :] for i in range(4))
        bm5 = sb("bm5", [P, NB], f32)
        lm5 = sb("lm5", [P, NB], f32)
        dcol = sb("dcol", [TE, TU], f32)
        dcol1 = sb("dcol1", [TE, TU], f32)
        scol = sb("scol", [TE, TU], f32)
        dint = sb("dint", [TE, 3, TU], i32)
        hif = sb("hif", [TE, 2, TU], f32)
        pos = sb("pos", [TE, TU], f32)
        rank = sb("rank", [TE, TU], f32)
        eqj = sb("eqj", [TE, UP, TE], bf16)
        Lq = sb("Lq", [P, 3, LO], f32)
        Tq = sb("Tq", [P, 1], f32)
        TM = sb("TM", [P, NB], f32)
        nt = sb("nt", [P, 4, NB], f32)
        nti = sb("nti", [P, 2, NB], i32)
        start = sb("start", [P, 1], f32)
        base2 = sb("base2", [P, LO], f32)
        blkf = sb("blkf", [1, 2, T + UN], f32)
        blk = sb("blk", [1, T + UN], i32)
        srcs = sb("srcs", [P, T + UN], i32)
        vcol = sb("vcol", [P, TP], f32)
        dloc_i = sb("dloc_i", [P, 2, T], i32)
        dloc = sb("dloc", [P, T], f32)
        dlT = sb("dlT", [P, 2, P], bf16)
        edge_ix = [sb(f"edge_ix{i}", [P, 1], i32) for i in range(UN)]
        ends = sb("ends", [P, 4], f32)
        rows = sb("rows", [1, 4, P], f32)
        carry_row = sb("carry_row", [1, 2, P + 1], f32)
        carry = sb("carry", [P, 2], f32)
        stats = sb("stats", [P, NB, 2, 6], f32)
        mv = sb("mv", [P, NB, 2], f32)
        std = sb("std", [P, NB], f32)
        rstd = sb("rstd", [P, NB], f32)
        nmr = sb("nmr", [P, NB], f32)
        rden = sb("rden", [P, NB, H], f32)

        ps = ctx.enter_context(nc.psum_tensor("ps", [P, 4096], f32))
        slot = [ps[:, 2048:2048 + D], ps[:, 3072:3072 + D]]
        psz = [ps[:, i * 1024:i * 1024 + FW] for i in range(3)]
        ps_cnt = ps[:, 512:512 + Q * LO]
        ps_ohT = ps[:, 0:512].bitcast(bf16).rearrange("p (q e) -> p q e", e=P)
        ps_perm = ps[:, 512:512 + 2 * T]
        ps_lt = ps[:, 512:512 + L]

        s_load = sem("s_load")
        s_x = sem("s_x")
        s_wk = [sem(f"s_wk{k}") for k in range(KC)]
        s_wu = sem("s_wu")
        s_rows = sem("s_rows")
        s_attn = sem("s_attn")
        s_drow = [sem("s_drow0"), sem("s_drow1")]
        s_const = sem("s_const")
        s_dve = sem("s_dve")
        s_ident = sem("s_ident")
        s_rawf = sem("s_rawf")
        s_cols = sem("s_cols")
        s_oh = sem("s_oh")
        s_cnt = sem("s_cnt")
        s_oht = sem("s_oht")
        s_ohte = sem("s_ohte")
        s_lq = sem("s_lq")
        s_base = sem("s_base")
        s_tab = sem("s_tab")
        s_look = sem("s_look")
        s_sel = sem("s_sel")
        s_rank = sem("s_rank")
        s_perm = sem("s_perm")
        s_permd = sem("s_permd")
        s_zero = sem("s_zero")
        s_sorted = sem("s_sorted")
        s_dlt = sem("s_dlt")
        s_dlte = sem("s_dlte")
        s_dlw = sem("s_dlw")
        s_dlb = sem("s_dlb")
        s_vrep = sem("s_vrep")
        s_vt = sem("s_vt")
        s_vs = sem("s_vs")
        s_vse = sem("s_vse")
        s_edges = sem("s_edges")
        s_h = sem("s_h")
        s_pp = sem("s_pp")
        s_pe = sem("s_pe")
        s_fb = sem("s_fb")
        s_um = sem("s_um")
        s_fu = sem("s_fu")
        s_tw = [sem("s_tw0"), sem("s_tw1")]
        s_hi = sem("s_hi")
        s_r1 = sem("s_r1")
        s_mid = sem("s_mid")
        s_fd = sem("s_fd")
        s_clear = sem("s_clear")
        s_ix = sem("s_ix")
        s_g = [sem(f"s_g{i}") for i in range(UN)]
        s_z = sem("s_z")
        s_add = sem("s_add")
        s_relu = sem("s_relu")
        s_u = sem("s_u")
        s_mul = sem("s_mul")
        s_red = sem("s_red")
        s_lg = sem("s_lg")
        s_lt = sem("s_lt")
        s_en = sem("s_en")
        s_er = sem("s_er")
        s_cr = sem("s_cr")
        s_ca = sem("s_ca")
        s_m = sem("s_m")
        s_ex = sem("s_ex")
        s_et = sem("s_et")
        s_exd = sem("s_exd")
        s_oha = sem("s_oha")
        s_wg = sem("s_wg")
        s_agg = sem("s_agg")
        s_lnr = sem("s_lnr")
        s_min = sem("s_min")
        s_exm = sem("s_exm")
        s_var = sem("s_var")
        s_std = sem("s_std")
        s_ln = sem("s_ln")
        s_nrm = sem("s_nrm")
        s_res = sem("s_res")
        s_out = sem("s_out")

        block = ctx.enter_context(nc.Block())
        attn_in = [attn1.rearrange("h d -> (h d)"), attno.rearrange("h d -> (h d)")]
        bvec = [[b1s, b1d], [bos, bod]]
        wmat = [[W1s, W1d], [Wos, Wod]]
        lnv = [(ln1_w, ln1_b), (lno_w, lno_b)]

        def row(v):
            return v.rearrange("(a n) -> a n", a=1)

        @block.sync
        def _(sp):
            for v, e in enumerate((dst, src)):
                sp.dma_start(raw[:, 2 * v:2 * v + 2, :], e.rearrange("(a q p) -> q a p", a=2, p=TE)
                             ).then_inc(s_load, 16)
            for c in range(2):
                sp.dma_start(dst_row[c], row(dst)[:, c * CE:(c + 1) * CE].partition_broadcast(TE)
                             ).then_inc(s_drow[c], 16)
            for b in range(NB):
                n = min(P, N - b * P)
                if n < P:
                    sp.wait_ge(s_zero, 1)
                sp.dma_start(h0[0:n, b, :], x[b * P:b * P + n, :]).then_inc(s_x, 16)
            for c in range(2, CHUNK):
                sp.wait_ge(s_rank, (c - 1) * CTU)
                sp.dma_start(dst_row[c % 2], row(dst)[:, c * CE:(c + 1) * CE].partition_broadcast(TE)
                             ).then_inc(s_drow[c % 2], 16)

            def table_out(layer):
                for b in range(NB):
                    sp.wait_ge(s_fu, layer * 2 * NB + b + 1)
                    sp.dma_start(tables[layer][b * P:(b + 1) * P, :], ftile[b % 2][:, :]).then_inc(s_tw[b % 2], 16)

            table_out(0)
            sp.wait_ge(s_dlte, 2)
            sp.dma_start(dl_rows[0:P, :], dlT[:, 0, :]).then_inc(s_dlw, 16)
            sp.dma_start(dl_rows[P:T, :], dlT[0:T - P, 1, :]).then_inc(s_dlw, 16)
            sp.wait_ge(s_dlw, 32)
            sp.dma_start(onehotT, dl_rows.rearrange("(a t) p -> a (t p)", a=1).partition_broadcast(P)
                         ).then_inc(s_dlb, 16)
            table_out(1)
            sp.wait_ge(s_pp, 2 * len(PROJ))
            for b in range(NB):
                n = min(P, N - b * P)
                sp.dma_start(Wm[0:n, b, :], x[b * P:b * P + n, :]).then_inc(s_x, 16)
            for b in range(NB):
                n = min(P, N - b * P)
                sp.wait_ge(s_res, b + 1)
                sp.dma_start(out[b * P:b * P + n, :], h0[0:n, b, :]).then_inc(s_out, 16)
            sp.wait_ge(s_out, NB * 16)

        @block.gpsimd
        def _(pool):
            def iota(o, pattern, base, mult):
                pool.iota(o, pattern, base=base, channel_multiplier=mult,
                          allow_small_or_imprecise_dtypes=True).then_inc(s_const, 1)
            iota(diff[:, :], [[1, P]], 0, -1)
            iota(iota_t[:, :], [[1, T + UN]], 0, 0)
            iota(iota_p[:, :], [[0, 1]], 0, 1)
            iota(ci[:, 0, :], [[1, P]], 0, 0)
            iota(pi[:, 0:1], [[0, 1]], 0, 1)
            pool.memset(h0[:, NB - 1, :], 0.0).then_inc(s_zero, 1)

            def project(layer):
                pool.wait_ge(s_rows, (layer + 1) * 48)
                pool.wait_ge(s_attn, layer + 1)
                for u in range(2 * NB):
                    n, f, b = layer * 2 * NB + u, ftile[u % 2], u % NB
                    i = PROJ.index(("FD"[u // NB], b))
                    pool.wait_ge(s_pe, layer * len(PROJ) + i + 1)
                    pool.tensor_tensor(f[:, 0:D], f[:, 0:D], bias[u // NB][:, :], ALU.add).then_inc(s_fb, 1)
                    pool.wait_ge(s_fb, n + 1)
                    if n:
                        pool.wait_ge(s_fu, n)
                    pool.tensor_tensor(utmp[:, :], f[:, 0:D], attn_row[:, :], ALU.mult).then_inc(s_um, 1)
                    if u >= NB:
                        m, o = layer * NB + b + 1, b * FW
                        pool.wait_ge(s_hi, m)
                        pool.tensor_tensor(f[:, :], f[:, :], FD[0][:, o:o + FW], ALU.subtract).then_inc(s_r1, 1)
                        pool.wait_ge(s_mid, m)
                        pool.tensor_tensor(FD[2][:, o:o + FW], f[:, :], FD[1][:, o:o + FW], ALU.subtract).then_inc(s_fd, 1)

            def gather(layer, phase):
                turn = 2 * layer + phase
                free, before = ((s_add, layer * T), (s_wg, 0) if layer == 0 else (s_agg, T))[phase]
                if turn:
                    pool.wait_ge(s_ix, turn * (T + 1))
                pool.tensor_copy(edge_ix[0][:, :], srcs[:, 0:1]).then_inc(s_ix, 1)

                def step(s, j, k):
                    if live(s, 5):
                        pool.wait_ge(free, before + s - 4)
                    pool.wait_ge(s_ix, turn * (T + 1) + s + 1)
                    pool.tensor_copy(edge_ix[(j + 1) % UN][:, :], srcs[:, bass.ds(s + 1, 1)]).then_inc(s_ix, 1)
                    pool.indirect_dma_start(G[j], None, tables[layer],
                                            bass.IndirectOffsetOnAxis(ap=edge_ix[j][:, 0:1], axis=0)
                                            ).then_inc(s_g[j], 16)
                tiles(pool, step)

            for layer in range(2):
                project(layer)
                if layer == 0:
                    pool.wait_ge(s_edges, 1)
                else:
                    pool.wait_ge(s_ln, 2)
                pool.wait_ge(s_tw[0], (layer + 1) * 48)
                pool.wait_ge(s_tw[1], (layer + 1) * 32)
                gather(layer, 0)
                pool.wait_ge(s_exd, layer + 1)
                gather(layer, 1)

        @block.scalar
        def _(act):
            def weights(layer):
                for i in range(2):
                    for k in range(KC):
                        if i:
                            act.wait_ge(s_wu, (2 * layer + i - 1) * KC + k + 1)
                        act.dma_start(Wm[:, k, :], wmat[layer][i][k * P:(k + 1) * P, :]).then_inc(s_wk[k], 16)
                    yield

            def small_rows(layer):
                for i in range(2):
                    act.dma_start(bias[i][:, :], row(bvec[layer][i]).partition_broadcast(P)).then_inc(s_rows, 16)
                act.dma_start(attn_row[:, :], row(attn_in[layer]).partition_broadcast(P)).then_inc(s_rows, 16)
                act.wait_ge(s_rows, (layer + 1) * 48)
                act.activation(attn_row[:, :], attn_row[:, :], ACT.Copy, scale=1.0 - SLOPE).then_inc(s_attn, 1)

            def project(layer, loads):
                def post(u):
                    n, f, b = layer * 2 * NB + u, ftile[u % 2], u % NB
                    act.wait_ge(s_um, n + 1)
                    heads = H if layer == 0 else 1
                    w = D // heads
                    for h in range(heads):
                        last = act.activation(utmp[:, h * w:(h + 1) * w], utmp[:, h * w:(h + 1) * w], ACT.Copy,
                                              scale=SLOPE / (1.0 - SLOPE), accum_out=f[:, D + h:D + h + 1])
                    if heads < H:
                        last = act.activation(f[:, D + heads:FW], zerof[:, heads:H], ACT.Copy)
                    last.then_inc(s_fu, 1)
                    if u >= NB:
                        o = b * FW
                        act.wait_ge(s_fu, n + 1)
                        act.activation(FD[0][:, o:o + FW], f[:, :], ACT.Copy).then_inc(s_hi, 1)
                        act.wait_ge(s_r1, layer * NB + b + 1)
                        act.activation(FD[1][:, o:o + FW], f[:, :], ACT.Copy).then_inc(s_mid, 1)

                u = 0
                for i, (kind, b) in enumerate(PROJ):
                    act.wait_ge(s_pp, layer * len(PROJ) + i + 1)
                    if kind == "T":
                        act.activation(hT[:, :, b * P:(b + 1) * P], slot[i % 2].rearrange("p (k n) -> p k n", n=P),
                                       ACT.Copy).then_inc(s_pe, 1)
                        continue
                    if 2 <= u < NB + 2:
                        act.wait_ge(s_tw[u % 2], (layer * (3 - u % 2) + (u - 2) // 2 + 1) * 16)
                    elif u >= NB + 2:
                        act.wait_ge(s_fd, layer * NB + u - 2 - NB + 1)
                    act.activation(ftile[u % 2][:, 0:D], slot[i % 2], ACT.Copy).then_inc(s_pe, 1)
                    if u:
                        post(u - 1)
                    u += 1
                    if u == NB:
                        next(loads)
                post(u - 1)

            def scores(layer):
                def step(s, j, k):
                    act.wait_ge(s_add, layer * T + s + 1)
                    z = Z[j % 3]
                    act.activation(z[:, 0:D], z[:, 0:D], ACT.Relu).then_inc(s_relu, 1)
                    act.activation(ulog[:, bass.ds(s * H, H)], z[:, D:FW], ACT.Copy).then_inc(s_u, 1)
                tiles(act, step)

            def std_of(n):
                act.wait_ge(s_var, n + 1)
                act.activation(std[:, :], std[:, :], ACT.Sqrt).then_inc(s_std, 1)
                act.wait_ge(s_ln, n + 1)

            loads = weights(0)
            next(loads)
            small_rows(0)
            std_of(0)
            for b in range(NB):
                act.activation(h0[:, b, :], h0[:, b, :], ACT.Relu, bias=nmr[:, b:b + 1],
                               scale=rstd[:, b:b + 1]).then_inc(s_h, 1)
            for g in range(Q // 8):
                act.wait_ge(s_oht, g + 1)
                act.activation(OHT[:, g * 8:(g + 1) * 8, :], ps_ohT[:, :, 0:TE], ACT.Copy).then_inc(s_ohte, 1)
            for layer in range(2):
                project(layer, loads)
                act.wait_ge(s_clear, layer + 1)
                scores(layer)
                if layer == 0:
                    loads = weights(1)
                    next(loads)
                    act.wait_ge(s_red, T)
                    small_rows(1)
                act.wait_ge(s_m, layer + 1)
                act.activation(LT, LT, ACT.Exp).then_inc(s_ex, 1)
                act.wait_ge(s_agg, (layer + 1) * T)
                for v, r in zip(lnv[layer], (lnw_row, lnb_row)):
                    act.dma_start(r, row(v).partition_broadcast(P)).then_inc(s_lnr, 16)
                for b in range(NB):
                    n = layer * NB + b
                    act.wait_ge(s_min, n + 1)
                    act.activation(evac[2 + b % 2], evac[2 + b % 2], ACT.Exp).then_inc(s_exm, 1)
                std_of(layer + 1)
                for b in range(NB):
                    act.activation(h0[:, b, :], h0[:, b, :], ACT.Identity, bias=nmr[:, b:b + 1],
                                   scale=rstd[:, b:b + 1]).then_inc(s_nrm, 1)

        @block.vector
        def _(dve):
            own = [0]

            def link(ins):
                own[0] += 1
                ins.then_inc(s_dve, 1)
                dve.wait_ge(s_dve, own[0])

            def norm(n):
                for b in range(NB):
                    dve.bn_stats(stats[:, b, 0, :], h0[:, b, 0:D // 2])
                    link(dve.bn_stats(stats[:, b, 1, :], h0[:, b, D // 2:D]))
                    link(dve.bn_aggr(mv[:, b, :], stats[:, b, :, :].rearrange("p a c -> p (a c)")))
                dve.tensor_scalar(std[:, :], mv[:, :, 1], EPS, None, ALU.add).then_inc(s_var, 1)
                dve.wait_ge(s_std, n + 1)
                link(dve.reciprocal(rstd[:, :], std[:, :]))
                dve.scalar_tensor_tensor(nmr[:, :], mv[:, :, 0], -1.0, rstd[:, :], ALU.mult, ALU.mult).then_inc(s_ln, 1)

            dve.memset(zeros[:, :], 0.0)
            dve.memset(zerof[:, :], 0.0)
            dve.memset(ones[:, :], 1.0)
            dve.memset(carry_row[:, :, :], -BIG)
            dve.memset(srcs[:, :], 0)
            link(dve.memset(logits[:, 0:1], 0.0))
            dve.wait_ge(s_const, 5)
            dve.tensor_scalar(ident[:, :], diff[:, :], 0.0, None, ALU.is_equal)
            dve.tensor_scalar(identb[:, :], diff[:, :], 0.0, None, ALU.is_equal)
            dve.tensor_scalar(ltmask[:, :], diff[:, :], 0.0, None, ALU.is_lt)
            dve.tensor_scalar(shift_up[:, :], diff[:, :], float(H), None, ALU.is_equal)
            dve.tensor_scalar(shift_dn[:, :], diff[:, :], float(-H), None, ALU.is_equal)
            dve.tensor_copy(iota_h[:, :], iota_t[:, :])
            for m in (ci, pi):
                lo, hi, bl = (m[:, i, :] if m is ci else m[:, i:i + 1] for i in (1, 2, 3))
                a = m[:, 0, :] if m is ci else m[:, 0:1]
                dve.tensor_scalar(hi, a, 5, None, ALU.arith_shift_right)
                link(dve.tensor_scalar(lo, a, 31, None, ALU.bitwise_and))
                link(dve.tensor_scalar(bl, lo, 2, None, ALU.arith_shift_right))
            link(dve.tensor_copy(pf[:, :], pi[:, :]))
            lo_p, j_p, b_p = pf[:, 1:2], pf[:, 2:3], pf[:, 3:4]
            dve.tensor_scalar(Mhi, ci[:, 1, :], lo_p, None, ALU.is_equal)
            dve.tensor_scalar(Msame, ci[:, 3, :], b_p, None, ALU.is_equal)
            dve.tensor_scalar(bm5[:, :], iota_t[:, 0:NB], b_p, None, ALU.is_equal)
            link(dve.tensor_scalar(lm5[:, :], iota_t[:, 0:NB], b_p, None, ALU.is_lt))
            dve.scalar_tensor_tensor(Mj, ci[:, 2, :], j_p, Mhi, ALU.is_gt, ALU.mult)
            dve.scalar_tensor_tensor(Mless, ci[:, 1, :], lo_p, Msame, ALU.is_gt, ALU.mult).then_inc(s_ident, 1)

            dve.wait_ge(s_load, 32)
            dve.tensor_copy(rawf, raw).then_inc(s_rawf, 1)
            dve.wait_ge(s_cols, 1)
            dve.tensor_copy(scol[:, :], ps[0:TE, TU:2 * TU])
            dve.tensor_copy(dint[:, 0, :], ps[0:TE, 0:TU])
            link(dve.tensor_copy(dcol[:, :], ps[0:TE, 0:TU]))
            dve.tensor_scalar(dint[:, 1, :], dint[:, 0, :], 5, None, ALU.arith_shift_right)
            dve.tensor_scalar(dint[:, 2, :], dint[:, 0, :], 31, None, ALU.bitwise_and)
            link(dve.tensor_scalar(dcol1[:, :], dcol[:, :], 1.0, None, ALU.add))
            link(dve.tensor_copy(hif[:, :, :], dint[:, 1:3, :]))
            for o, part in ((OH, 0), (OL, 1)):
                dve.tensor_tensor(o, hif[:, part, :].unsqueeze(2).to_broadcast([TE, TU, LO]),
                                  iota_t[0:TE, 0:LO].unsqueeze(1).to_broadcast([TE, TU, LO]),
                                  ALU.is_equal).then_inc(s_oh, 1)

            dve.wait_ge(s_x, NB * 16)
            norm(0)

            dve.wait_ge(s_cnt, 1)
            ct3, tab3 = (m.rearrange("p (l q) -> p l q", l=LO) for m in (CT, TAB))
            link(dve.tensor_copy(ct3, ps_cnt.rearrange("p (q l) -> p l q", l=LO)))
            Lt, Lx, Li = Lq[:, 0, :], Lq[:, 1, :], Lq[:, 2, :]
            link(dve.tensor_reduce(Lt, ct3, AX.X, ALU.add))
            dve.tensor_reduce(Tq[:, :], Lt, AX.X, ALU.add)
            link(dve.tensor_tensor_scan(Li, Lt, zerof[:, :], 0.0, ALU.add, ALU.add))
            dve.tensor_scalar(TM[:, :], bm5[:, :], Tq[:, 0:1], None, ALU.mult)
            dve.tensor_tensor(Lx, Li, Lt, ALU.subtract).then_inc(s_lq, 1)
            link(dve.tensor_tensor_scan(TAB, CT, zerof[:, 0:1].to_broadcast([P, LO * Q]), 0.0, ALU.add, ALU.add))
            link(dve.tensor_tensor(TAB, TAB, CT, ALU.subtract))
            dve.wait_ge(s_base, 1)
            link(dve.tensor_scalar(nti[:, 0, :], ps[:, LO:LO + NB], float(P - 1), None, ALU.add))
            link(dve.tensor_scalar(nti[:, 1, :], nti[:, 0, :], 7, None, ALU.arith_shift_right))
            link(dve.tensor_copy(nt[:, 0, :], nti[:, 1, :]))
            dve.tensor_tensor_scan(nt[:, 1, :], nt[:, 0, :], zerof[:, 0:NB], 0.0, ALU.add, ALU.add)
            link(dve.tensor_tensor(nt[:, 2, :], nt[:, 0, :], lm5[:, :], ALU.mult))
            link(dve.tensor_reduce(nt[:, 3, 0:1], nt[:, 2, :], AX.X, ALU.add))
            link(dve.tensor_scalar(start[:, :], nt[:, 3, 0:1], float(P), None, ALU.mult))
            link(dve.scalar_tensor_tensor(base2[:, :], ps[:, 0:LO], start[:, 0:1], Lx, ALU.add, ALU.subtract))
            dve.tensor_tensor(tab3, tab3, base2[:, :].unsqueeze(2).to_broadcast([P, LO, Q]), ALU.add).then_inc(s_tab, 1)
            link(dve.tensor_scalar(blkf[:, 0, :], iota_t[0:1, :], nt[0:1, 1, 0:1], None, ALU.is_ge))
            for b in range(1, NB - 1):
                link(dve.scalar_tensor_tensor(blkf[:, b % 2, :], iota_t[0:1, :], nt[0:1, 1, b:b + 1],
                                              blkf[:, (b - 1) % 2, :], ALU.is_ge, ALU.add))
            link(dve.tensor_copy(blk[:, :], blkf[:, (NB - 2) % 2, :]))

            def rank_of(c, t, j):
                if live(t, UP, TU):
                    dve.wait_ge(s_rank, t - UP + 1)
                dve.scalar_tensor_tensor(eqj[:, j, :], dst_row[c % 2][:, bass.ds((t - c * CTU) * TE, TE)],
                                         dcol[:, bass.ds(t, 1)], ltmask[0:TE, 0:TE], ALU.is_equal, ALU.mult,
                                         accum_out=rank[:, bass.ds(t, 1)]).then_inc(s_rank, 1)
            for c in range(CHUNK):
                dve.wait_ge(s_drow[c % 2], (c // 2 + 1) * 16)
                if c == 0:
                    for j in range(UP):
                        rank_of(c, j, j)
                with dve.Fori(max(c * CTU, UP), (c + 1) * CTU - UP + 1, UP) as t:
                    for j in range(UP):
                        rank_of(c, t + j, j)

            def by_tile(m):
                return m.rearrange("p (r q j) -> p r j q", j=QJ, q=QG)
            for g in range(Q // QG):
                b = sel[g % 2].rearrange("p (j q l) -> p j q l", j=QJ, l=LO)
                banks = ps[0:TE, 2048 * (g % 2):2048 * (g % 2 + 1)].rearrange("p (j c) -> p j c", j=QJ)
                dve.wait_ge(s_look, g + 1)
                dve.tensor_tensor(b, banks[:, :, 0:QG * LO].rearrange("p j (q l) -> p j q l", l=LO),
                                  OL.rearrange("p (r q j) l -> p r j q l", j=QJ, q=QG)[:, g], ALU.mult).then_inc(s_sel, 1)
                dve.wait_ge(s_sel, g + 1)
                link(dve.tensor_reduce(by_tile(pos[:, :])[:, g], b, AX.X, ALU.add))
            dve.wait_ge(s_rank, TU)
            link(dve.tensor_tensor(dint[:, 0, :], pos[:, :], rank[:, :], ALU.add))
            dve.tensor_scalar(dint[:, 1, :], dint[:, 0, :], P - 1, None, ALU.bitwise_and)
            link(dve.tensor_scalar(dint[:, 2, :], dint[:, 0, :], 7, None, ALU.arith_shift_right))
            link(dve.tensor_copy(hif[:, :, :], dint[:, 1:3, :]))

            def permute(t, j, k):
                if live(t, UP, TU):
                    dve.wait_ge(s_permd, t - UP + 1)
                dve.tensor_scalar(perm_l[j], iota_h[0:TE, 0:P], hif[:, 0, bass.ds(t, 1)], None, ALU.is_equal)
                for v, col in enumerate((scol, dcol1)):
                    last = dve.tensor_scalar(perm_r[j][:, v * T:(v + 1) * T], iota_h[0:TE, 0:T],
                                             hif[:, 1, bass.ds(t, 1)], col[:, bass.ds(t, 1)], ALU.is_equal, ALU.mult)
                last.then_inc(s_perm, 1)
            tiles(dve, permute, n=TU, un=UP)

            dve.wait_ge(s_permd, TU)
            dve.tensor_copy(srcs[:, 0:T], ps_perm[:, 0:T])
            dve.memset(vcol[:, T:TP], 0.0)
            link(dve.tensor_copy(vcol[:, 0:T], ps_perm[:, T:2 * T]))
            dve.tensor_scalar(dloc_i[:, 0, :], vcol[:, 0:T], -1.0, None, ALU.add)
            link(dve.tensor_scalar(dloc[:, :], vcol[:, 0:T], 0.0, -1000.0, ALU.is_equal, ALU.mult))
            link(dve.tensor_scalar(dloc_i[:, 1, :], dloc_i[:, 0, :], P - 1, None, ALU.bitwise_and))
            link(dve.tensor_tensor(dloc[:, :], dloc[:, :], dloc_i[:, 1, :], ALU.add))
            dve.tensor_scalar(BWD.rearrange("p (a c h) -> p c a h", c=CH, h=H),
                              vcol[:, :].rearrange("p (c a) -> p c a", c=CH).unsqueeze(3).to_broadcast([P, CH, TC, H]),
                              1.0, None, ALU.add).then_inc(s_sorted, 1)
            dve.wait_ge(s_dlt, 1)
            dve.tensor_copy(dlT[:, 0, :], ps[:, 0:P]).then_inc(s_dlte, 1)
            dve.tensor_copy(dlT[0:T - P, 1, :], ps[0:T - P, P:2 * P]).then_inc(s_dlte, 1)
            dve.wait_ge(s_vt, 1)
            link(dve.tensor_copy(LT, ps_lt))
            dve.tensor_tensor(reset_f[:, 1:L], LT[:, 1:L], LT[:, 0:L - 1], ALU.not_equal)
            dve.tensor_tensor(reset_b[:, 0:L - 1], LT[:, 1:L], LT[:, 0:L - 1], ALU.not_equal).then_inc(s_vs, 1)
            dve.wait_ge(s_vse, 1)
            dve.tensor_tensor(reset_f[:, 0:1], LT[:, 0:1], ps[:, 256:257], ALU.not_equal)
            link(dve.tensor_tensor(reset_b[:, L - 1:L], LT[:, L - 1:L], ps[:, 257:258], ALU.not_equal))
            dve.tensor_scalar(reset_f, reset_f, -BIG, None, ALU.mult)
            link(dve.tensor_scalar(reset_b, reset_b, -BIG, None, ALU.mult))
            dve.tensor_reduce(ends[:, 0:1], reset_f, AX.X, ALU.add)
            dve.tensor_reduce(ends[:, 1:2], reset_b, AX.X, ALU.add).then_inc(s_vs, 1)
            dve.wait_ge(s_vse, 2)
            for i in range(2):
                link(dve.tensor_copy(rows[:, i, :].rearrange("a (h c) -> a c h", h=H),
                                     ps[0:1, i * P:(i + 1) * P].rearrange("a (c h) -> a c h", h=H)))
            dve.wait_ge(s_dlb, 16)
            for c in range(4):
                w = T * P // 4
                last = dve.tensor_scalar(onehotT[:, c * w:(c + 1) * w], onehotT[:, c * w:(c + 1) * w],
                                         iota_p[:, 0:1], None, ALU.is_equal)
            last.then_inc(s_edges, 1)

            def scores(layer):
                def add(s, j, k):
                    dve.wait_ge(s_g[j], (2 * layer * UK + k + 1) * 16)
                    dve.wait_ge(s_z, layer * T + s + 1)
                    if live(s, 3):
                        dve.wait_ge(s_u, layer * T + s - 2)
                        dve.wait_ge(s_mul, layer * T + s - 2)
                    dve.tensor_tensor(Z[j % 3], G[j], psz[j % 3], ALU.add).then_inc(s_add, 1)

                def times(s, j):
                    dve.wait_ge(s_relu, layer * T + s)
                    if live(s, 3):
                        dve.wait_ge(*((s_red, s - 2) if layer == 0 else (s_mul, T + s - 2)))
                    j = (j - 1) % UN
                    if layer == 0:
                        dve.tensor_tensor(Y[j % 2], Z[j % 3][:, 0:D], attn_row[:, :], ALU.mult).then_inc(s_mul, 1)
                    else:
                        dve.scalar_tensor_tensor(Y[j % 2], Z[j % 3][:, 0:D], 1.0, attn_row[:, :], ALU.mult, ALU.mult,
                                                 accum_out=logits[:, bass.ds((s - 1) * H, 1)]).then_inc(s_mul, 1)

                def reduce(s, j):
                    dve.wait_ge(s_mul, layer * T + s - 1)
                    dve.tensor_reduce(logits[:, bass.ds((s - 2) * H, H)],
                                      Y[j % 2].rearrange("p (h d) -> p h d", h=H), AX.X, ALU.add).then_inc(s_red, 1)

                def step(s, j, k):
                    if live(s, 0):
                        add(s, j, k)
                    if live(s, 1):
                        times(s, j)
                    if layer == 0 and live(s, 2):
                        reduce(s, j)
                tiles(dve, step, lag=2 if layer == 0 else 1)

            def softmax(layer):
                dve.wait_ge(s_u, (layer + 1) * T)
                dve.wait_ge(s_mul, (layer + 1) * T)
                if layer == 0:
                    dve.wait_ge(s_red, T)
                dve.tensor_tensor(*(m.rearrange(f"p ({o} h) -> p c a h", c=CH, h=H) for m, o in
                                    ((BWD, "a c"), (logits, "c a"), (ulog, "c a"))), ALU.add).then_inc(s_lg, 1)
                dve.wait_ge(s_lt, layer + 1)
                link(dve.tensor_copy(LT, ps_lt))
                dve.tensor_tensor_scan(FWD, reset_f, LT, -BIG, ALU.add, ALU.max)
                dve.tensor_tensor_scan(BWD[:, ::-1], reset_b[:, ::-1], LT[:, ::-1], -BIG, ALU.add,
                                       ALU.max).then_inc(s_en, 1)
                dve.wait_ge(s_er, layer + 1)
                for i in range(2):
                    link(dve.tensor_copy(rows[:, 2 + i, :].rearrange("a (h c) -> a c h", h=H),
                                         ps[0:1, i * P:(i + 1) * P].rearrange("a (c h) -> a c h", h=H)))
                dve.tensor_tensor_scan(carry_row[:, 0, 1:P + 1], rows[:, 0, :], rows[:, 2, :], -BIG, ALU.add, ALU.max)
                link(dve.tensor_tensor_scan(carry_row[:, 1, 0:P][:, ::-1], rows[:, 1, ::-1], rows[:, 3, ::-1], -BIG,
                                            ALU.add, ALU.max))
                for i in range(2):
                    last = dve.tensor_copy(rows[:, 2 + i, :].rearrange("a (c h) -> a c h", h=H),
                                           carry_row[:, i, i:i + P].rearrange("a (h c) -> a c h", h=H))
                last.then_inc(s_cr, 1)
                dve.wait_ge(s_ca, layer + 1)
                link(dve.tensor_copy(carry[:, :], ps[:, 256:258]))
                dve.tensor_tensor_scan(FWD, reset_f, LT, carry[:, 0:1], ALU.add, ALU.max)
                link(dve.tensor_tensor_scan(BWD[:, ::-1], reset_b[:, ::-1], LT[:, ::-1], carry[:, 1:2], ALU.add,
                                            ALU.max))
                link(dve.tensor_tensor(FWD, FWD, BWD, ALU.max))
                dve.tensor_tensor(LT, LT, FWD, ALU.subtract).then_inc(s_m, 1)
                dve.wait_ge(s_et, layer + 1)
                dve.tensor_copy(logits.rearrange("p (c a h) -> p a c h", c=CH, h=H),
                                ps_lt.rearrange("p (a c h) -> p a c h", c=CH, h=H)).then_inc(s_exd, 1)
                dve.wait_ge(s_exd, layer + 1)

            def aggregate(layer):
                def step(s, j, k):
                    if live(s, 3):
                        dve.wait_ge(s_agg, layer * T + s - 2)
                    if layer == 0:
                        dve.tensor_scalar(oh_agg[j % 3], iota_t[:, 0:P], dloc[:, bass.ds(s, 1)], None,
                                          ALU.is_equal).then_inc(s_oha, 1)
                        dve.wait_ge(s_g[j], (UK + k + 1) * 16)
                        dve.tensor_tensor(WG[j % 3].rearrange("p (h d) -> p h d", h=H),
                                          G[j][:, 0:D].rearrange("p (h d) -> p h d", h=H),
                                          logits[:, bass.ds(s * H, H)].unsqueeze(2).to_broadcast([P, H, HD]),
                                          ALU.mult).then_inc(s_wg, 1)
                    else:
                        dve.tensor_scalar(oh_agg[j % 3], iota_t[:, 0:P], dloc[:, bass.ds(s, 1)],
                                          logits[:, bass.ds(s * H, 1)], ALU.is_equal, ALU.mult).then_inc(s_oha, 1)
                tiles(dve, step)

            def finish(layer):
                dve.wait_ge(s_agg, (layer + 1) * T)
                link(dve.tensor_scalar(rden[:, :, :].rearrange("p b h -> p (b h)"), ps[:, DEN:DEN + NB * H], 1e-30,
                                       None, ALU.max))
                link(dve.reciprocal(rden[:, :, :], rden[:, :, :]))
                for b in range(NB):
                    v, m = evac[b % 2], evac[2 + b % 2]
                    heads = H if layer == 0 else 1
                    link(dve.tensor_tensor(v.rearrange("p (h d) -> p h d", h=heads),
                                           ps[:, b * D:(b + 1) * D].rearrange("p (h d) -> p h d", h=heads),
                                           rden[:, b, 0:heads].unsqueeze(2).to_broadcast([P, heads, D // heads]),
                                           ALU.mult))
                    dve.tensor_scalar(m, v, 0.0, None, ALU.min).then_inc(s_min, 1)
                    dve.wait_ge(s_exm, layer * NB + b + 1)
                    link(dve.scalar_tensor_tensor(v, v, 0.0, m, ALU.max, ALU.add))
                    if layer == 0:
                        link(dve.scalar_tensor_tensor(h0[:, b, :], v, -1.0, h0[:, b, :], ALU.add, ALU.add))
                    else:
                        link(dve.tensor_scalar(h0[:, b, :], v, -1.0, None, ALU.add))
                norm(layer + 1)
                dve.wait_ge(s_lnr, (layer + 1) * 32)
                for b in range(NB):
                    dve.wait_ge(s_nrm, layer * NB + b + 1)
                    link(dve.tensor_tensor(h0[:, b, :], h0[:, b, :], lnw_row, ALU.mult))
                    if layer == 0:
                        dve.tensor_tensor(h0[:, b, :], h0[:, b, :], lnb_row, ALU.add).then_inc(s_h, 1)
                    else:
                        link(dve.tensor_tensor(h0[:, b, :], h0[:, b, :], lnb_row, ALU.add))
                        dve.wait_ge(s_x, 2 * NB * 16)
                        n = min(P, N - b * P)
                        dve.tensor_tensor(h0[0:n, b, :], h0[0:n, b, :], Wm[0:n, b, :], ALU.add).then_inc(s_res, 1)

            for layer in range(2):
                dve.wait_ge(s_fd, (layer + 1) * NB)
                dve.memset(R3[:, 0:2 * TP * H], 0.0).then_inc(s_clear, 1)
                dve.wait_ge(s_clear, layer + 1)
                scores(layer)
                softmax(layer)
                aggregate(layer)
                finish(layer)

        @block.tensor
        def _(pe):
            pe.wait_ge(s_ident, 1)
            pe.wait_ge(s_rawf, 1)
            for v in range(4):
                last = pe.transpose(ps[0:TE, v * 80:(v + 1) * 80], rawf[:, v, :], ident[0:80, 0:80])
            last.then_inc(s_cols, 1)
            pe.wait_ge(s_oh, 2)
            for t in range(TU):
                q, j = t // QJ, t % QJ
                last = pe.matmul(ps_cnt[32 * j:32 * j + 32, q * LO:(q + 1) * LO], OH[:, t, :], OL[:, t, :],
                                 start=True, stop=True)
            last.then_inc(s_cnt, 1)
            for g in range(Q // 8):
                if g:
                    pe.wait_ge(s_ohte, g)
                for q in range(8):
                    t = (g * 8 + q) * QJ
                    last = pe.transpose(ps_ohT[:, q, 0:TE], OH[:, t:t + QJ, :].rearrange("p t l -> p (t l)"),
                                        identb[0:TE, 0:TE])
                last.then_inc(s_oht, 1)
            pe.wait_ge(s_ohte, Q // 8)
            pe.wait_ge(s_lq, 1)
            pe.matmul(ps[:, 0:LO], Mhi, Lq[:, 1, :], start=True, stop=False)
            pe.matmul(ps[:, 0:LO], Mj, Lq[:, 0, :], start=False, stop=False)
            pe.matmul(ps[:, 0:LO], Mless, Tq[:, 0:1].to_broadcast([P, LO]), start=False, stop=True)
            pe.matmul(ps[:, LO:LO + NB], ones[:, :], TM[:, :], start=True, stop=True).then_inc(s_base, 1)
            pe.wait_ge(s_tab, 1)
            for g in range(Q // QG):
                if g >= 2:
                    pe.wait_ge(s_sel, g - 1)
                for q in range(QG):
                    for j in range(QJ):
                        qq, at = g * QG + q, 2048 * (g % 2) + 512 * j + q * LO
                        last = pe.matmul(ps[0:TE, at:at + LO], OHT[32 * j:32 * j + 32, qq, :],
                                         TAB[32 * j:32 * j + 32, qq::Q], start=True, stop=True)
                last.then_inc(s_look, 1)

            def project(layer):
                for i, (kind, b) in enumerate(PROJ):
                    n = layer * len(PROJ) + i
                    if n >= 2:
                        pe.wait_ge(s_pe, n - 1)
                    o = slot[i % 2]
                    if kind == "T":
                        pe.wait_ge(s_h, layer * NB + b + 1)
                        for k in range(KC):
                            last = pe.transpose(o[:, k * P:(k + 1) * P], h0[:, b, k * P:(k + 1) * P], ident[:, :])
                    else:
                        pe.wait_ge(s_pe, layer * len(PROJ) + PROJ.index(("T", b)) + 1)
                        v = 2 * layer + (kind == "D")
                        for k in range(KC):
                            pe.wait_ge(s_wk[k], (v + 1) * 16)
                            for c0, c1 in ((0, 512), (512, D)):
                                last = pe.matmul(o[:, c0:c1], hT[:, k, b * P:(b + 1) * P], Wm[:, k, c0:c1],
                                                 start=k == 0, stop=k == KC - 1)
                            if b == NB - 1 and k < KC - 1:
                                last.then_inc(s_wu, 1)
                    last.then_inc(s_pp, 1)
                    if kind != "T" and b == NB - 1:
                        pe.wait_ge(s_pp, n + 1)
                        pe.sem_inc(s_wu, 1)

            def scores(layer):
                def step(s, j, k):
                    b = pe.value_load(blk[0:1, bass.ds(s, 1)], min_val=0, max_val=NB - 1)
                    if live(s, 3):
                        pe.wait_ge(s_add, layer * T + s - 2)
                    for part in range(3):
                        for c0, c1 in ((0, 512), (512, FW)):
                            last = pe.matmul(psz[j % 3][:, c0:c1], onehotT[:, bass.ds(s * P, P)],
                                             FD[part][:, bass.ds(b * FW + c0, c1 - c0)],
                                             start=part == 0, stop=part == 2)
                    last.then_inc(s_z, 1)
                tiles(pe, step)

            def softmax(layer):
                pe.wait_ge(s_lg, layer + 1)
                for a in range(TC):
                    last = pe.transpose(ps_lt[:, a * P:(a + 1) * P], BWD[:, a * P:(a + 1) * P], ident[:, :])
                last.then_inc(s_lt, 1)
                pe.wait_ge(s_en, layer + 1)
                pe.transpose(ps[0:1, 0:P], FWD[:, L - 1:L], ident[:, :])
                pe.transpose(ps[0:1, P:2 * P], BWD[:, 0:1], ident[:, :]).then_inc(s_er, 1)
                pe.wait_ge(s_cr, layer + 1)
                pe.transpose(ps[:, 256:257], rows[:, 2, :], ident[0:1, 0:1])
                pe.transpose(ps[:, 257:258], rows[:, 3, :], ident[0:1, 0:1]).then_inc(s_ca, 1)
                pe.wait_ge(s_ex, layer + 1)
                for a in range(TC):
                    last = pe.transpose(ps_lt[:, a * P:(a + 1) * P], LT[:, a * P:(a + 1) * P], ident[:, :])
                last.then_inc(s_et, 1)

            def aggregate(layer):
                pe.wait_ge(s_exd, layer + 1)
                for b in range(8):
                    pe.matmul(ps[:, b * 512:(b + 1) * 512], zeros[:, 0:P], zeros[:, :], start=True, stop=True,
                              skip_group_check=True)

                def step(s, j, k):
                    b = pe.value_load(blk[0:1, bass.ds(s, 1)], min_val=0, max_val=NB - 1)
                    pe.wait_ge(s_oha, layer * T + s + 1)
                    if layer == 0:
                        pe.wait_ge(s_wg, s + 1)
                        rhs, den = WG[j % 3], logits[:, bass.ds(s * H, H)]
                    else:
                        pe.wait_ge(s_g[j], (3 * UK + k + 1) * 16)
                        rhs, den = G[j], ones[:, 0:H]
                    for c in range(D // HB):
                        pe.matmul(ps[:, bass.ds(b * D + c * HB, HB)], oh_agg[j % 3], rhs[:, c * HB:(c + 1) * HB],
                                  start=False, stop=False, skip_group_check=True)
                    pe.matmul(ps[:, bass.ds(DEN + b * H, H)], oh_agg[j % 3], den,
                              start=False, stop=False, skip_group_check=True).then_inc(s_agg, 1)
                tiles(pe, step)

            pe.wait_ge(s_sel, Q // QG)
            project(0)
            pe.matmul(ps[:, 512:1024], zeros[:, 0:P], zeros[:, :], start=True, stop=True, skip_group_check=True)

            def permute(t, j, k):
                pe.wait_ge(s_perm, t + 1)
                pe.matmul(ps_perm, perm_l[j], perm_r[j], start=False, stop=False,
                          skip_group_check=True).then_inc(s_permd, 1)
            tiles(pe, permute, n=TU, un=UP)
            pe.wait_ge(s_sorted, 1)
            pe.transpose(ps[:, 0:P], dloc[:, 0:P], ident[:, :])
            pe.transpose(ps[0:T - P, P:2 * P], dloc[:, P:T], ident[:, :]).then_inc(s_dlt, 1)
            for a in range(TC):
                last = pe.transpose(ps_lt[:, a * P:(a + 1) * P], BWD[:, a * P:(a + 1) * P], ident[:, :])
            last.then_inc(s_vt, 1)
            pe.wait_ge(s_vs, 1)
            pe.matmul(ps[:, 256:257], shift_up[:, :], LT[:, L - 1:L], start=True, stop=True)
            pe.matmul(ps[:, 257:258], shift_dn[:, :], LT[:, 0:1], start=True, stop=True).then_inc(s_vse, 1)
            pe.wait_ge(s_dlte, 2)
            pe.wait_ge(s_vs, 2)
            pe.transpose(ps[0:1, 0:P], ends[:, 0:1], ident[:, :])
            pe.transpose(ps[0:1, P:2 * P], ends[:, 1:2], ident[:, :]).then_inc(s_vse, 1)
            pe.wait_ge(s_edges, 1)
            for layer in range(2):
                if layer:
                    project(1)
                pe.wait_ge(s_fd, (layer + 1) * NB)
                scores(layer)
                softmax(layer)
                aggregate(layer)


INS = ["x", "src", "dst", "L0_gnn_W1s", "L0_gnn_b1s", "L0_gnn_W1d", "L0_gnn_b1d", "L0_gnn_attn1",
       "L0_gnn_ln1_w", "L0_gnn_ln1_b", "L0_gnn_Wos", "L0_gnn_bos", "L0_gnn_Wod", "L0_gnn_bod",
       "L0_gnn_attno", "L0_gnn_lno_w", "L0_gnn_lno_b"]


def kernel(**inputs):
    import numpy as np
    import concourse.bacc as bacc
    from concourse.bass_utils import run_bass_kernel_spmd

    nc = bacc.Bacc("TRN2", target_bir_lowering=False, num_devices=1)
    arrays, args = {}, []
    for name in INS:
        a = np.ascontiguousarray(inputs[name])
        arrays[f"in_{name}"] = a
        args.append(nc.dram_tensor(f"in_{name}", a.shape, mybir.dt.from_np(a.dtype), kind="ExternalInput").ap())
    args.append(nc.dram_tensor("out_0", (N, D), f32, kind="ExternalOutput").ap())
    gnn_program(nc, *args)
    r = run_bass_kernel_spmd(nc, [arrays], core_ids=[0])
    return r.results[0]["out_0"]
```

```python
import concourse.bass as bass
from concourse import mybir
from contextlib import ExitStack


P = 128
N = 625
NB = 5
NP = NB * P
D = 768
H = 8
HD = D // H
KC = D // P
E = 20000
TE = 125
TU = E // TE
QJ = 4
Q = TU // QJ
LO = 32
UN = 9
GI = 3
UI = 2 * UN
HA = 2
LU = 5
T = 162
assert T * P >= E + NB * (P - 1) and T % UI == 0
UK = T // UN
CH = 16
TC = 11
TP = CH * TC
L = TC * P
FW = D + H
EPS = 1e-5
SLOPE = 0.2
BIG = 1e30
HB = 256
DEN = NB * D
CHUNK = 4
CE = E // CHUNK
CTU = TU // CHUNK
UR = 8
UE = 4
UP = 8
PT = TU // NB
QG = 8

f32 = mybir.dt.float32
bf16 = mybir.dt.bfloat16
f16 = mybir.dt.float16
i32 = mybir.dt.int32
ALU = mybir.AluOpType
ACT = mybir.ActivationFunctionType
AX = mybir.AxisListType


PROJ = [("T", 0), ("T", 1), ("F", 0), ("T", 2), ("F", 1), ("T", 3), ("F", 2), ("T", 4),
        ("F", 3), ("F", 4), ("D", 0), ("D", 1), ("D", 2), ("D", 3), ("D", 4)]
PART = {("F", 4): 0, ("D", 0): 1, ("D", 1): 2, ("D", 2): 3, ("D", 3): 4}


def live(s, back, n=T):
    return not isinstance(s, int) or 0 <= s - back < n


def tiles(eng, body, lag=0, n=T, un=UN, first=0):
    if first == 0:
        for s in range(un):
            body(s, s, 0)
    with eng.Fori(max(first // un, 1), n // un) as k:
        for j in range(un):
            body(k * un + j, j, k)
    for s in range(n, n + lag):
        body(s, s % un, s // un)



def gnn_program(nc, x, src, dst, W1s, b1s, W1d, b1d, attn1, ln1_w, ln1_b,
                Wos, bos, Wod, bod, attno, lno_w, lno_b, out):
    ctx = ExitStack()
    with ctx:
        def sb(name, shape, dt):
            return ctx.enter_context(nc.sbuf_tensor(name, shape, dt))

        def sem(name):
            return ctx.enter_context(nc.semaphore(name))

        tables = [nc.dram_tensor(f"fs_table{l}", (NP, FW), f32, kind="Internal").ap() for l in range(2)]
        dl_rows = nc.dram_tensor("dl_rows", (T, P), bf16, kind="Internal").ap()

        R1 = sb("R1", [P, T * P // 2], f32)
        onehotT = R1[:, :].bitcast(bf16)
        dst_row = [R1[0:TE, c * CE:(c + 1) * CE].bitcast(i32) for c in range(2)]
        GW, YW = UN * FW, 3 * D + 3 * P
        R2W = max(GW + YW + 2 * L, TU * LO + Q * TE + 2 * Q * LO)
        R2 = sb("R2", [P, R2W], f32)
        G = [R2[:, i * FW:(i + 1) * FW] for i in range(UN)]
        Y = [R2[:, GW + i * D:GW + (i + 1) * D] for i in range(3)]
        WG = Y
        oh_agg = [R2[:, GW + 3 * D + i * P:GW + 3 * D + (i + 1) * P] for i in range(3)]
        reset_f = R2[:, R2W - 2 * L:R2W - L]
        reset_b = R2[:, R2W - L:R2W]
        LT, FWD, BWD = (R2[:, i * L:(i + 1) * L] for i in range(3))
        assert 3 * L <= GW
        evac = [R2[:, i * D:(i + 1) * D] for i in range(4)]
        lnw_row, lnb_row = (R2[:, (4 + i) * D:(5 + i) * D] for i in range(2))
        OH = R2[0:TE, 0:TU * LO // 2].bitcast(bf16).rearrange("p (t l) -> p t l", l=LO)
        OL = R2[0:TE, TU * LO // 2:TU * LO].bitcast(bf16).rearrange("p (t l) -> p t l", l=LO)
        OHT = R2[:, TU * LO:TU * LO + Q * TE].rearrange("p (q e) -> p q e", e=TE)
        raw = R2[0:80, TU * LO:TU * LO + 4 * TE].bitcast(i32).rearrange("q (v p) -> q v p", p=TE)
        rawf = R2[0:80, TU * LO + 4 * TE:TU * LO + 8 * TE].rearrange("q (v p) -> q v p", p=TE)
        CT = R2[:, TU * LO + Q * TE:TU * LO + Q * TE + Q * LO]
        TAB = R2[:, TU * LO + Q * TE + Q * LO:TU * LO + Q * TE + 2 * Q * LO]
        sel = [R2[0:TE, i * QJ * QG * LO:(i + 1) * QJ * QG * LO] for i in range(2)]
        perm_l = [[R2[0:TE, i * P // 2:(i + 1) * P // 2].bitcast(f16) for i in range(u, u + 3)]
                  for u in range(0, 3 * UP, 3)]
        at = 3 * UP * P // 2
        perm_r = [R2[0:TE, at + i * T // 2:at + (i + 1) * T // 2].bitcast(f16) for i in range(UP)]
        assert at + UP * T // 2 <= TU * LO // 2

        h0 = sb("h0", [P, NB, D], f32)
        R3 = sb("R3", [P, KC * NP], f32)
        hT = R3[:, :].rearrange("p (k n) -> p k n", k=KC)
        logits = R3[:, 0:TP * H]
        ulog = R3[:, TP * H:2 * TP * H]
        assert 2 * TP * H <= KC * NP
        Wm = sb("Wm", [P, KC, D], f32)
        bias = [sb(f"bias{i}", [P, D], f32) for i in range(2)]
        attn_row = sb("attn_row", [P, D], f32)
        FD = [sb(f"FD{i}", [P, NB * FW], bf16) for i in range(3)]
        ftile = [sb(f"ftile{i}", [P, FW], f32) for i in range(2)]
        utmp = sb("utmp", [P, D], f32)

        QD = FW * NB // 2 // P
        diag = [FD[q // QD][:, :].bitcast(f32)[:, q % QD * P:(q % QD + 1) * P] for q in range(Q)]

        ident = sb("ident", [P, P], f32)
        identb = sb("identb", [P, P], bf16)
        diff = sb("diff", [P, P], f32)
        ltmask = sb("ltmask", [P, P], f32)
        shift_up = sb("shift_up", [P, P], f32)
        shift_dn = sb("shift_dn", [P, P], f32)
        iota_t = sb("iota_t", [P, T + UN], f32)
        iota_h = sb("iota_h", [P, T + UN], f16)
        iota_p = sb("iota_p", [P, 1], f32)
        zeros = sb("zeros", [P, 512], bf16)
        zerof = sb("zerof", [P, LO], f32)
        ones = sb("ones", [P, P], f32)
        ci = sb("ci", [P, 4, P], i32)
        pi = sb("pi", [P, 4], i32)
        pf = sb("pf", [P, 4], f32)
        M = sb("M", [P, 5, P], f32)
        Mhi, Mj, Mless, Msame, Mgroup = (M[:, i, :] for i in range(5))
        bm5 = sb("bm5", [P, NB], f32)
        lm5 = sb("lm5", [P, NB], f32)
        dcol = sb("dcol", [TE, TU], f32)
        dcol1 = sb("dcol1", [TE, TU], f32)
        scol = sb("scol", [TE, TU], f32)
        dint = sb("dint", [TE, 3, TU], i32)
        hif = sb("hif", [TE, 2, TU], f32)
        pos = sb("pos", [TE, TU], f32)
        rank = sb("rank", [TE, TU], f32)
        eqj = sb("eqj", [TE, UE, TE], bf16)
        Lq = sb("Lq", [P, 3, LO], f32)
        Tq = sb("Tq", [P, 1], f32)
        TM = sb("TM", [P, NB], f32)
        nt = sb("nt", [P, 4, NB], f32)
        nti = sb("nti", [P, 2, NB], i32)
        start = sb("start", [P, 1], f32)
        base2 = sb("base2", [P, LO], f32)
        blkf = sb("blkf", [1, 2, T + UN], f32)
        blk = sb("blk", [1, T + UN], i32)
        srcs = sb("srcs", [P, T + UN], i32)
        vcol = sb("vcol", [P, TP], f32)
        dloc_i = sb("dloc_i", [P, 2, T], i32)
        dloc = sb("dloc", [P, T], f32)
        dlT = sb("dlT", [P, 2, P], bf16)
        edge_ix = sb("edge_ix", [P, UI], i32)
        ends = sb("ends", [P, 4], f32)
        rows = sb("rows", [1, 4, P], f32)
        carry_row = sb("carry_row", [1, 2, P + 1], f32)
        carry = sb("carry", [P, 2], f32)
        stats = sb("stats", [P, NB, 2, 6], f32)
        mv = sb("mv", [P, NB, 2], f32)
        std = sb("std", [P, NB], f32)
        rstd = sb("rstd", [P, NB], f32)
        nmr = sb("nmr", [P, NB], f32)
        rden = sb("rden", [P, NB, H], f32)

        ps = ctx.enter_context(nc.psum_tensor("ps", [P, 4096], f32))
        slot = [ps[:, 2048:2048 + D], ps[:, 3072:3072 + D]]
        psz = [ps[:, i * 1024:i * 1024 + FW] for i in range(3)]
        ps_cnt = ps[:, 512:512 + Q * LO]
        ps_ohT = ps[:, 0:512].bitcast(bf16).rearrange("p (q e) -> p q e", e=P)
        ps_perm = ps[:, 512:512 + 2 * T]
        ps_lt = ps[:, 512:512 + L]

        s_load = sem("s_load")
        s_x = sem("s_x")
        s_wk = [sem(f"s_wk{k}") for k in range(KC)]
        s_wu = sem("s_wu")
        s_rows = sem("s_rows")
        s_attn = sem("s_attn")
        s_drow = [sem("s_drow0"), sem("s_drow1")]
        s_const = sem("s_const")
        s_dve = sem("s_dve")
        s_ident = sem("s_ident")
        s_rawf = sem("s_rawf")
        s_cols = sem("s_cols")
        s_oh = sem("s_oh")
        s_cnt = sem("s_cnt")
        s_oht = sem("s_oht")
        s_ohte = sem("s_ohte")
        s_lq = sem("s_lq")
        s_base = sem("s_base")
        s_look = sem("s_look")
        s_sel = sem("s_sel")
        s_rank = sem("s_rank")
        s_diag = sem("s_diag")
        s_perm = sem("s_perm")
        s_scaled0 = sem("s_scaled0")
        s_scaled1 = sem("s_scaled1")
        s_permd = sem("s_permd")
        s_zero = sem("s_zero")
        s_sorted = sem("s_sorted")
        s_dlt = sem("s_dlt")
        s_dlte = sem("s_dlte")
        s_dlw = sem("s_dlw")
        s_dlb = sem("s_dlb")
        s_vrep = sem("s_vrep")
        s_vt = sem("s_vt")
        s_vs = sem("s_vs")
        s_vse = sem("s_vse")
        s_edges = sem("s_edges")
        s_h = sem("s_h")
        s_pp = sem("s_pp")
        s_pe = sem("s_pe")
        s_fb = sem("s_fb")
        s_um = sem("s_um")
        s_fu = sem("s_fu")
        s_tw = [sem("s_tw0"), sem("s_tw1")]
        s_hi = sem("s_hi")
        s_r1 = sem("s_r1")
        s_mid = sem("s_mid")
        s_fd = sem("s_fd")
        s_clear = sem("s_clear")
        s_ix = sem("s_ix")
        s_gs = [sem(f"s_gs{i}") for i in range(UN)]
        s_ga = [sem(f"s_ga{i}") for i in range(UN)]
        s_z = sem("s_z")
        s_zc = sem("s_zc")
        s_u = sem("s_u")
        s_mul = sem("s_mul")
        s_red = sem("s_red")
        s_reda = sem("s_reda")
        s_lg = sem("s_lg")
        s_lt = sem("s_lt")
        s_en = sem("s_en")
        s_er = sem("s_er")
        s_cr = sem("s_cr")
        s_ca = sem("s_ca")
        s_m = sem("s_m")
        s_ex = sem("s_ex")
        s_et = sem("s_et")
        s_exd = sem("s_exd")
        s_oha = sem("s_oha")
        s_wg = sem("s_wg")
        s_agg = sem("s_agg")
        s_lnr = sem("s_lnr")
        s_min = sem("s_min")
        s_exm = sem("s_exm")
        s_var = sem("s_var")
        s_std = sem("s_std")
        s_ln = sem("s_ln")
        s_nrm = sem("s_nrm")
        s_res = sem("s_res")
        s_out = sem("s_out")

        block = ctx.enter_context(nc.Block())
        attn_in = [attn1.rearrange("h d -> (h d)"), attno.rearrange("h d -> (h d)")]
        bvec = [[b1s, b1d], [bos, bod]]
        wmat = [[W1s, W1d], [Wos, Wod]]
        lnv = [(ln1_w, ln1_b), (lno_w, lno_b)]

        def row(v):
            return v.rearrange("(a n) -> a n", a=1)

        @block.sync
        def _(sp):
            for v, e in enumerate((dst, src)):
                sp.dma_start(raw[:, 2 * v:2 * v + 2, :], e.rearrange("(a q p) -> q a p", a=2, p=TE)
                             ).then_inc(s_load, 16)

            def drow(c):
                sp.dma_start(dst_row[c % 2], row(dst)[:, c * CE:(c + 1) * CE].partition_broadcast(TE)
                             ).then_inc(s_drow[c % 2], 16)

            drow(0)
            for b in range(NB):
                n = min(P, N - b * P)
                if n < P:
                    sp.wait_ge(s_zero, 1)
                sp.dma_start(h0[0:n, b, :], x[b * P:b * P + n, :]).then_inc(s_x, 16)
            drow(1)
            for c in range(2, CHUNK):
                sp.wait_ge(s_rank, (c - 1) * CTU)
                drow(c)

            def table_out(layer):
                for b in range(NB):
                    sp.wait_ge(s_fu, layer * 2 * NB + b + 1)
                    sp.dma_start(tables[layer][b * P:(b + 1) * P, :], ftile[b % 2][:, :]).then_inc(s_tw[b % 2], 16)

            table_out(0)
            sp.wait_ge(s_dlte, 2)
            sp.dma_start(dl_rows[0:P, :], dlT[:, 0, :]).then_inc(s_dlw, 16)
            sp.dma_start(dl_rows[P:T, :], dlT[0:T - P, 1, :]).then_inc(s_dlw, 16)
            sp.wait_ge(s_dlw, 32)
            sp.dma_start(onehotT, dl_rows.rearrange("(a t) p -> a (t p)", a=1).partition_broadcast(P)
                         ).then_inc(s_dlb, 16)
            table_out(1)
            sp.wait_ge(s_pp, 2 * len(PROJ))
            for b in range(NB):
                n = min(P, N - b * P)
                sp.dma_start(Wm[0:n, b, :], x[b * P:b * P + n, :]).then_inc(s_x, 16)
            for b in range(NB):
                n = min(P, N - b * P)
                sp.wait_ge(s_res, b + 1)
                sp.dma_start(out[b * P:b * P + n, :], h0[0:n, b, :]).then_inc(s_out, 16)
            sp.wait_ge(s_out, NB * 16)

        @block.gpsimd
        def _(pool):
            def iota(o, pattern, base, mult):
                pool.iota(o, pattern, base=base, channel_multiplier=mult,
                          allow_small_or_imprecise_dtypes=True).then_inc(s_const, 1)
            iota(diff[:, :], [[1, P]], 0, -1)
            iota(iota_t[:, :], [[1, T + UN]], 0, 0)
            iota(iota_p[:, :], [[0, 1]], 0, 1)
            iota(ci[:, 0, :], [[1, P]], 0, 0)
            iota(pi[:, 0:1], [[0, 1]], 0, 1)
            pool.memset(h0[:, NB - 1, :], 0.0).then_inc(s_zero, 1)

            def permute(c):
                def step(t, j, k):
                    pool.wait_ge(s_perm, t + 1)
                    if live(t, UP, TU):
                        pool.wait_ge(s_permd, t - UP + 1)
                    pool.tensor_tensor(perm_l[j][2], perm_l[j][0], dcol1[:, bass.ds(t, 1)].to_broadcast([TE, P]),
                                       ALU.mult).then_inc(s_scaled1, 1)
                tiles(pool, step, n=(c + 1) * PT, un=UP, first=c * PT)

            def project(layer):
                parts = [[PART[PROJ[i + 1]] for i in range(PROJ.index(("FD"[u // NB], u % NB)) + 1)
                          if i + 1 < len(PROJ) and PROJ[i + 1] in PART
                          and (u == 0 or i > PROJ.index(("FD"[(u - 1) // NB], (u - 1) % NB)))]
                         for u in range(2 * NB)]
                pool.wait_ge(s_rows, (layer + 1) * 48)
                pool.wait_ge(s_attn, layer + 1)
                for u in range(2 * NB):
                    n, f, b = layer * 2 * NB + u, ftile[u % 2], u % NB
                    i = PROJ.index(("FD"[u // NB], b))
                    for part in parts[u] if layer == 0 else []:
                        permute(part)
                    pool.wait_ge(s_pe, layer * len(PROJ) + i + 1)
                    pool.tensor_tensor(f[:, 0:D], f[:, 0:D], bias[u // NB][:, :], ALU.add).then_inc(s_fb, 1)
                    pool.wait_ge(s_fb, n + 1)
                    if n:
                        pool.wait_ge(s_fu, n)
                    pool.tensor_tensor(utmp[:, :], f[:, 0:D], attn_row[:, :], ALU.mult).then_inc(s_um, 1)
                    if u >= NB:
                        m, o = layer * NB + b + 1, b * FW
                        pool.wait_ge(s_hi, m)
                        pool.tensor_tensor(f[:, :], f[:, :], FD[0][:, o:o + FW], ALU.subtract).then_inc(s_r1, 1)
                        pool.wait_ge(s_mid, m)
                        pool.tensor_tensor(FD[2][:, o:o + FW], f[:, :], FD[1][:, o:o + FW], ALU.subtract).then_inc(s_fd, 1)

            def gather(layer, phase):
                turn = 2 * layer + phase
                used, before = (s_wg, 0) if layer == 0 else (s_agg, T)
                if turn:
                    pool.wait_ge(s_ix, turn * (T // GI + 1))
                pool.tensor_copy(edge_ix[:, 0:GI], srcs[:, 0:GI]).then_inc(s_ix, 1)

                def step(s, j, k):
                    if j % GI == 0:
                        pool.wait_ge(s_ix, turn * (T // GI + 1) + k * (UI // GI) + j // GI + 1)
                        if phase == 0:
                            pool.wait_ge(s_zc, layer * T + s + GI)
                        elif live(s + GI - 1, UN):
                            pool.wait_ge(used, before + s + GI - UN)
                        at = (j + GI) % UI
                        pool.tensor_copy(edge_ix[:, at:at + GI], srcs[:, bass.ds(s + GI, GI)]).then_inc(s_ix, 1)
                    pool.indirect_dma_start(G[j % UN], None, tables[layer],
                                            bass.IndirectOffsetOnAxis(ap=edge_ix[:, j:j + 1], axis=0),
                                            compute_op=(ALU.add, ALU.bypass)[phase]
                                            ).then_inc((s_gs, s_ga)[phase][j % UN], 16)
                tiles(pool, step, un=UI)

            for layer in range(2):
                project(layer)
                if layer == 0:
                    pool.wait_ge(s_edges, 1)
                else:
                    pool.wait_ge(s_ln, 2)
                pool.wait_ge(s_tw[0], (layer + 1) * 48)
                pool.wait_ge(s_tw[1], (layer + 1) * 32)
                gather(layer, 0)
                pool.wait_ge(s_exd, layer + 1)
                gather(layer, 1)

        @block.scalar
        def _(act):
            def weights(layer):
                for i in range(2):
                    for k in range(KC):
                        if i:
                            act.wait_ge(s_wu, (2 * layer + i - 1) * KC + k + 1)
                        act.dma_start(Wm[:, k, :], wmat[layer][i][k * P:(k + 1) * P, :]).then_inc(s_wk[k], 16)
                    yield

            def small_rows(layer):
                for i in range(2):
                    act.dma_start(bias[i][:, :], row(bvec[layer][i]).partition_broadcast(P)).then_inc(s_rows, 16)
                act.dma_start(attn_row[:, :], row(attn_in[layer]).partition_broadcast(P)).then_inc(s_rows, 16)
                act.wait_ge(s_rows, (layer + 1) * 48)
                act.activation(attn_row[:, :], attn_row[:, :], ACT.Copy, scale=1.0 - SLOPE).then_inc(s_attn, 1)

            def project(layer, loads):
                def post(u):
                    n, f, b = layer * 2 * NB + u, ftile[u % 2], u % NB
                    act.wait_ge(s_um, n + 1)
                    heads = H if layer == 0 else 1
                    w = D // heads
                    for h in range(heads):
                        last = act.activation(utmp[:, h * w:(h + 1) * w], utmp[:, h * w:(h + 1) * w], ACT.Copy,
                                              scale=SLOPE / (1.0 - SLOPE), accum_out=f[:, D + h:D + h + 1])
                    if heads < H:
                        last = act.activation(f[:, D + heads:FW], zerof[:, heads:H], ACT.Copy)
                    last.then_inc(s_fu, 1)
                    if u >= NB:
                        o = b * FW
                        act.wait_ge(s_fu, n + 1)
                        act.activation(FD[0][:, o:o + FW], f[:, :], ACT.Copy).then_inc(s_hi, 1)
                        act.wait_ge(s_r1, layer * NB + b + 1)
                        act.activation(FD[1][:, o:o + FW], f[:, :], ACT.Copy).then_inc(s_mid, 1)

                u, waiting = 0, None
                for i, (kind, b) in enumerate(PROJ):
                    if layer == 0 and PROJ[min(i + 1, len(PROJ) - 1)] in PART:
                        if waiting is not None:
                            post(waiting)
                            waiting = None
                        permute(PART[PROJ[i + 1]])
                    act.wait_ge(s_pp, layer * len(PROJ) + i + 1)
                    if kind == "T":
                        act.activation(hT[:, :, b * P:(b + 1) * P], slot[i % 2].rearrange("p (k n) -> p k n", n=P),
                                       ACT.Copy).then_inc(s_pe, 1)
                        continue
                    if 2 <= u < NB + 2:
                        act.wait_ge(s_tw[u % 2], (layer * (3 - u % 2) + (u - 2) // 2 + 1) * 16)
                    elif u >= NB + 2:
                        act.wait_ge(s_fd, layer * NB + u - 2 - NB + 1)
                    act.activation(ftile[u % 2][:, 0:D], slot[i % 2], ACT.Copy).then_inc(s_pe, 1)
                    if waiting is not None:
                        post(waiting)
                    waiting = u
                    u += 1
                    if u == NB:
                        next(loads)
                post(waiting)

            def permute(c):
                def step(t, j, k):
                    act.wait_ge(s_perm, t + 1)
                    if live(t, UP, TU):
                        act.wait_ge(s_permd, t - UP + 1)
                    act.activation(perm_l[j][1], perm_l[j][0], ACT.Copy,
                                   scale=scol[:, bass.ds(t, 1)]).then_inc(s_scaled0, 1)
                tiles(act, step, n=(c + 1) * PT, un=UP, first=c * PT)

            def scores(layer):
                def copy(s, j):
                    act.wait_ge(s_z, layer * T + s + 1)
                    if live(s, UN):
                        act.wait_ge(s_mul, layer * T + s - UN + 1)
                        act.wait_ge(s_u, layer * T + s - UN + 1)
                    act.activation(G[j], psz[j % 3], ACT.Copy).then_inc(s_zc, 1)

                def linear(s, j, k):
                    act.wait_ge(s_gs[j], (layer * (T // UN) + k + 1) * 16)
                    act.activation(ulog[:, bass.ds(s * H, H)], G[j][:, D:FW], ACT.Copy).then_inc(s_u, 1)

                def heads(s, j):
                    act.wait_ge(s_mul, s + 1)
                    for h in range(H - HA, H):
                        y = Y[j % 3][:, h * HD:(h + 1) * HD]
                        last = act.activation(y, y, ACT.Copy, accum_out=logits[:, bass.ds(s * H + h, 1)])
                    last.then_inc(s_reda, 1)

                def step(s, j, k):
                    if live(s, 0):
                        copy(s, j)
                    if live(s, LU):
                        linear(s - LU, (j - LU) % UN, k - (j < LU))
                    if layer == 0 and live(s, LU + 1):
                        heads(s - LU - 1, (j - LU - 1) % UN)
                tiles(act, step, lag=LU + 1)

            def std_of(n):
                act.wait_ge(s_var, n + 1)
                act.activation(std[:, :], std[:, :], ACT.Sqrt).then_inc(s_std, 1)
                act.wait_ge(s_ln, n + 1)

            loads = weights(0)
            next(loads)
            small_rows(0)
            for g in range(Q // 8):
                act.wait_ge(s_oht, g + 1)
                act.activation(OHT[:, g * 8:(g + 1) * 8, :], ps_ohT[:, :, 0:TE], ACT.Copy).then_inc(s_ohte, 1)
            std_of(0)
            for b in range(NB):
                act.activation(h0[:, b, :], h0[:, b, :], ACT.Relu, bias=nmr[:, b:b + 1],
                               scale=rstd[:, b:b + 1]).then_inc(s_h, 1)
            for layer in range(2):
                project(layer, loads)
                act.wait_ge(s_clear, layer + 1)
                scores(layer)
                if layer == 0:
                    loads = weights(1)
                    next(loads)
                    act.wait_ge(s_mul, T)
                    small_rows(1)
                act.wait_ge(s_m, layer + 1)
                act.activation(LT, LT, ACT.Exp).then_inc(s_ex, 1)
                act.wait_ge(s_agg, (layer + 1) * T)
                for v, r in zip(lnv[layer], (lnw_row, lnb_row)):
                    act.dma_start(r, row(v).partition_broadcast(P)).then_inc(s_lnr, 16)
                for b in range(NB):
                    n = layer * NB + b
                    act.wait_ge(s_min, n + 1)
                    act.activation(evac[2 + b % 2], evac[2 + b % 2], ACT.Exp).then_inc(s_exm, 1)
                std_of(layer + 1)
                for b in range(NB):
                    act.activation(h0[:, b, :], h0[:, b, :], ACT.Identity, bias=nmr[:, b:b + 1],
                                   scale=rstd[:, b:b + 1]).then_inc(s_nrm, 1)

        @block.vector
        def _(dve):
            own = [0]

            def link(ins):
                own[0] += 1
                ins.then_inc(s_dve, 1)
                dve.wait_ge(s_dve, own[0])

            def moments(b):
                dve.bn_stats(stats[:, b, 0, :], h0[:, b, 0:D // 2])
                link(dve.bn_stats(stats[:, b, 1, :], h0[:, b, D // 2:D]))
                link(dve.bn_aggr(mv[:, b, :], stats[:, b, :, :].rearrange("p a c -> p (a c)")))

            def norm(n):
                dve.tensor_scalar(std[:, :], mv[:, :, 1], EPS, None, ALU.add).then_inc(s_var, 1)
                dve.wait_ge(s_std, n + 1)
                link(dve.reciprocal(rstd[:, :], std[:, :]))
                dve.scalar_tensor_tensor(nmr[:, :], mv[:, :, 0], -1.0, rstd[:, :], ALU.mult, ALU.mult).then_inc(s_ln, 1)

            dve.memset(zeros[:, :], 0.0)
            dve.memset(zerof[:, :], 0.0)
            dve.memset(ones[:, :], 1.0)
            dve.memset(carry_row[:, :, :], -BIG)
            dve.memset(srcs[:, :], 0)
            link(dve.memset(logits[:, 0:1], 0.0))
            dve.wait_ge(s_const, 5)
            dve.tensor_scalar(ident[:, :], diff[:, :], 0.0, None, ALU.is_equal)
            dve.tensor_scalar(identb[:, :], diff[:, :], 0.0, None, ALU.is_equal)
            dve.tensor_scalar(ltmask[:, :], diff[:, :], 0.0, None, ALU.is_lt)
            dve.tensor_scalar(shift_up[:, :], diff[:, :], float(H), None, ALU.is_equal)
            dve.tensor_scalar(shift_dn[:, :], diff[:, :], float(-H), None, ALU.is_equal)
            dve.tensor_copy(iota_h[:, :], iota_t[:, :])
            for m in (ci, pi):
                lo, hi, bl = (m[:, i, :] if m is ci else m[:, i:i + 1] for i in (1, 2, 3))
                a = m[:, 0, :] if m is ci else m[:, 0:1]
                dve.tensor_scalar(hi, a, 5, None, ALU.arith_shift_right)
                link(dve.tensor_scalar(lo, a, 31, None, ALU.bitwise_and))
                link(dve.tensor_scalar(bl, lo, 2, None, ALU.arith_shift_right))
            link(dve.tensor_copy(pf[:, :], pi[:, :]))
            lo_p, j_p, b_p = pf[:, 1:2], pf[:, 2:3], pf[:, 3:4]
            dve.tensor_scalar(Mhi, ci[:, 1, :], lo_p, None, ALU.is_equal)
            dve.tensor_scalar(Mgroup, ci[:, 2, :], j_p, None, ALU.is_equal)
            dve.tensor_scalar(Msame, ci[:, 3, :], b_p, None, ALU.is_equal)
            dve.tensor_scalar(bm5[:, :], iota_t[:, 0:NB], b_p, None, ALU.is_equal)
            link(dve.tensor_scalar(lm5[:, :], iota_t[:, 0:NB], b_p, None, ALU.is_lt))
            dve.scalar_tensor_tensor(Mj, ci[:, 2, :], j_p, Mhi, ALU.is_gt, ALU.mult)
            dve.scalar_tensor_tensor(Mless, ci[:, 1, :], lo_p, Msame, ALU.is_gt, ALU.mult).then_inc(s_ident, 1)

            dve.wait_ge(s_load, 32)
            dve.tensor_copy(rawf, raw).then_inc(s_rawf, 1)
            dve.wait_ge(s_cols, 1)
            dve.tensor_copy(scol[:, :], ps[0:TE, TU:2 * TU])
            dve.tensor_copy(dint[:, 0, :], ps[0:TE, 0:TU])
            link(dve.tensor_copy(dcol[:, :], ps[0:TE, 0:TU]))
            dve.tensor_scalar(dint[:, 1, :], dint[:, 0, :], 5, None, ALU.arith_shift_right)
            dve.tensor_scalar(dint[:, 2, :], dint[:, 0, :], 31, None, ALU.bitwise_and)
            link(dve.tensor_scalar(dcol1[:, :], dcol[:, :], 1.0, None, ALU.add))
            link(dve.tensor_copy(hif[:, :, :], dint[:, 1:3, :]))
            for o, part in ((OH, 0), (OL, 1)):
                dve.tensor_tensor(o, hif[:, part, :].unsqueeze(2).to_broadcast([TE, TU, LO]),
                                  iota_t[0:TE, 0:LO].unsqueeze(1).to_broadcast([TE, TU, LO]),
                                  ALU.is_equal).then_inc(s_oh, 1)

            def ranks(c):
                def rank_of(t, j):
                    if j % 2 == 0 and live(t, UE, TU):
                        dve.wait_ge(s_rank, t - UE + 2)
                    dve.scalar_tensor_tensor(eqj[:, j % UE, :], dst_row[c % 2][:, bass.ds((t - c * CTU) * TE, TE)],
                                             dcol[:, bass.ds(t, 1)], ltmask[0:TE, 0:TE], ALU.is_equal, ALU.mult,
                                             accum_out=rank[:, bass.ds(t, 1)]).then_inc(s_rank, 1)
                dve.wait_ge(s_drow[c % 2], (c // 2 + 1) * 16)
                if c == 0:
                    for j in range(UR):
                        rank_of(j, j)
                with dve.Fori(max(c * CTU, UR), (c + 1) * CTU - UR + 1, UR) as t:
                    for j in range(UR):
                        rank_of(t + j, j)
            ranks(0)

            dve.wait_ge(s_cnt, 1)
            ct3, tab3 = (m.rearrange("p (l q) -> p l q", l=LO) for m in (CT, TAB))
            link(dve.tensor_copy(ct3, ps_cnt.rearrange("p (q l) -> p l q", l=LO)))
            Lt, Lx, Li = Lq[:, 0, :], Lq[:, 1, :], Lq[:, 2, :]
            link(dve.tensor_reduce(Lt, ct3, AX.X, ALU.add))
            dve.tensor_reduce(Tq[:, :], Lt, AX.X, ALU.add)
            link(dve.tensor_tensor_scan(Li, Lt, zerof[:, :], 0.0, ALU.add, ALU.add))
            dve.tensor_scalar(TM[:, :], bm5[:, :], Tq[:, 0:1], None, ALU.mult)
            dve.tensor_tensor(Lx, Li, Lt, ALU.subtract).then_inc(s_lq, 1)
            link(dve.tensor_tensor_scan(TAB, CT, zerof[:, 0:1].to_broadcast([P, LO * Q]), 0.0, ALU.add, ALU.add))
            link(dve.tensor_tensor(TAB, TAB, CT, ALU.subtract))
            dve.wait_ge(s_base, 1)
            link(dve.tensor_scalar(nti[:, 0, :], ps[:, LO:LO + NB], float(P - 1), None, ALU.add))
            link(dve.tensor_scalar(nti[:, 1, :], nti[:, 0, :], 7, None, ALU.arith_shift_right))
            link(dve.tensor_copy(nt[:, 0, :], nti[:, 1, :]))
            dve.tensor_tensor_scan(nt[:, 1, :], nt[:, 0, :], zerof[:, 0:NB], 0.0, ALU.add, ALU.add)
            link(dve.tensor_tensor(nt[:, 2, :], nt[:, 0, :], lm5[:, :], ALU.mult))
            link(dve.tensor_reduce(nt[:, 3, 0:1], nt[:, 2, :], AX.X, ALU.add))
            link(dve.tensor_scalar(start[:, :], nt[:, 3, 0:1], float(P), None, ALU.mult))
            link(dve.scalar_tensor_tensor(base2[:, :], ps[:, 0:LO], start[:, 0:1], Lx, ALU.add, ALU.subtract))
            link(dve.tensor_tensor(tab3, tab3, base2[:, :].unsqueeze(2).to_broadcast([P, LO, Q]), ALU.add))
            for g in range(Q // QG):
                for q in range(g * QG, (g + 1) * QG):
                    last = dve.tensor_tensor(diag[q].rearrange("p (j l) -> p j l", j=QJ),
                                             TAB[:, q::Q].unsqueeze(1).to_broadcast([P, QJ, LO]),
                                             Mgroup.rearrange("p (j l) -> p j l", j=QJ), ALU.mult)
                last.then_inc(s_diag, 1)
            link(dve.tensor_scalar(blkf[:, 0, :], iota_t[0:1, :], nt[0:1, 1, 0:1], None, ALU.is_ge))
            for b in range(1, NB - 1):
                link(dve.scalar_tensor_tensor(blkf[:, b % 2, :], iota_t[0:1, :], nt[0:1, 1, b:b + 1],
                                              blkf[:, (b - 1) % 2, :], ALU.is_ge, ALU.add))
            link(dve.tensor_copy(blk[:, :], blkf[:, (NB - 2) % 2, :]))

            def select(g):
                w, tt = QG * QJ * LO, slice(g * QG * QJ, (g + 1) * QG * QJ)
                dve.wait_ge(s_look, g + 1)
                dve.tensor_tensor(sel[g % 2], ps[0:TE, w * (g % 4):w * (g % 4 + 1)],
                                  OL[:, tt, :].rearrange("p t l -> p (t l)"), ALU.mult).then_inc(s_sel, 1)
                dve.wait_ge(s_sel, g + 1)
                link(dve.tensor_reduce(pos[:, tt], sel[g % 2].rearrange("p (t l) -> p t l", l=LO), AX.X, ALU.add))

            dve.wait_ge(s_x, NB * 16)
            for b in range(3):
                moments(b)
            select(0)
            select(1)
            moments(3)
            moments(4)
            norm(0)
            select(2)
            select(3)
            select(4)
            for c in range(1, CHUNK):
                ranks(c)
            dve.wait_ge(s_rank, TU)
            link(dve.tensor_tensor(dint[:, 0, :], pos[:, :], rank[:, :], ALU.add))
            dve.tensor_scalar(dint[:, 1, :], dint[:, 0, :], P - 1, None, ALU.bitwise_and)
            link(dve.tensor_scalar(dint[:, 2, :], dint[:, 0, :], 7, None, ALU.arith_shift_right))
            link(dve.tensor_copy(hif[:, :, :], dint[:, 1:3, :]))

            def permute(t, j, k):
                if live(t, UP, TU):
                    dve.wait_ge(s_permd, t - UP + 1)
                dve.tensor_scalar(perm_l[j][0], iota_h[0:TE, 0:P], hif[:, 0, bass.ds(t, 1)], None, ALU.is_equal)
                dve.tensor_scalar(perm_r[j], iota_h[0:TE, 0:T], hif[:, 1, bass.ds(t, 1)], None,
                                  ALU.is_equal).then_inc(s_perm, 1)
            tiles(dve, permute, n=TU, un=UP)

            dve.wait_ge(s_permd, TU)
            dve.tensor_copy(srcs[:, 0:T], ps_perm[:, 0:T])
            dve.memset(vcol[:, T:TP], 0.0)
            link(dve.tensor_copy(vcol[:, 0:T], ps_perm[:, T:2 * T]))
            dve.tensor_scalar(dloc_i[:, 0, :], vcol[:, 0:T], -1.0, None, ALU.add)
            link(dve.tensor_scalar(dloc[:, :], vcol[:, 0:T], 0.0, -1000.0, ALU.is_equal, ALU.mult))
            link(dve.tensor_scalar(dloc_i[:, 1, :], dloc_i[:, 0, :], P - 1, None, ALU.bitwise_and))
            link(dve.tensor_tensor(dloc[:, :], dloc[:, :], dloc_i[:, 1, :], ALU.add))
            dve.tensor_scalar(BWD.rearrange("p (a c h) -> p c a h", c=CH, h=H),
                              vcol[:, :].rearrange("p (c a) -> p c a", c=CH).unsqueeze(3).to_broadcast([P, CH, TC, H]),
                              1.0, None, ALU.add).then_inc(s_sorted, 1)
            dve.wait_ge(s_dlt, 1)
            dve.tensor_copy(dlT[:, 0, :], ps[:, 0:P]).then_inc(s_dlte, 1)
            dve.tensor_copy(dlT[0:T - P, 1, :], ps[0:T - P, P:2 * P]).then_inc(s_dlte, 1)
            dve.wait_ge(s_vt, 1)
            link(dve.tensor_copy(LT, ps_lt))
            dve.tensor_tensor(reset_f[:, 1:L], LT[:, 1:L], LT[:, 0:L - 1], ALU.not_equal)
            dve.tensor_tensor(reset_b[:, 0:L - 1], LT[:, 1:L], LT[:, 0:L - 1], ALU.not_equal).then_inc(s_vs, 1)
            dve.wait_ge(s_vse, 1)
            dve.tensor_tensor(reset_f[:, 0:1], LT[:, 0:1], ps[:, 256:257], ALU.not_equal)
            link(dve.tensor_tensor(reset_b[:, L - 1:L], LT[:, L - 1:L], ps[:, 257:258], ALU.not_equal))
            dve.tensor_scalar(reset_f, reset_f, -BIG, None, ALU.mult)
            link(dve.tensor_scalar(reset_b, reset_b, -BIG, None, ALU.mult))
            dve.tensor_reduce(ends[:, 0:1], reset_f, AX.X, ALU.add)
            dve.tensor_reduce(ends[:, 1:2], reset_b, AX.X, ALU.add).then_inc(s_vs, 1)
            dve.wait_ge(s_vse, 2)
            for i in range(2):
                link(dve.tensor_copy(rows[:, i, :].rearrange("a (h c) -> a c h", h=H),
                                     ps[0:1, i * P:(i + 1) * P].rearrange("a (c h) -> a c h", h=H)))
            dve.wait_ge(s_dlb, 16)
            for c in range(4):
                w = T * P // 4
                last = dve.tensor_scalar(onehotT[:, c * w:(c + 1) * w], onehotT[:, c * w:(c + 1) * w],
                                         iota_p[:, 0:1], None, ALU.is_equal)
            last.then_inc(s_edges, 1)

            def scores(layer):
                def times(s, j, k):
                    dve.wait_ge(s_gs[j], (layer * (T // UN) + k + 1) * 16)
                    if live(s, 3):
                        if layer == 0:
                            dve.wait_ge(s_red, s - 2)
                            dve.wait_ge(s_reda, s - 2)
                        else:
                            dve.wait_ge(s_mul, T + s - 2)
                    dve.scalar_tensor_tensor(Y[j % 3], G[j][:, 0:D], 0.0, attn_row[:, :], ALU.max, ALU.mult,
                                             accum_out=logits[:, bass.ds(s * H, 1)] if layer else None
                                             ).then_inc(s_mul, 1)

                def sums(s, j):
                    dve.wait_ge(s_mul, layer * T + s + 1)
                    dve.tensor_reduce(logits[:, bass.ds(s * H, H - HA)],
                                      Y[j % 3][:, 0:(H - HA) * HD].rearrange("p (h d) -> p h d", d=HD),
                                      AX.X, ALU.add).then_inc(s_red, 1)

                def step(s, j, k):
                    if live(s, 0):
                        times(s, j, k)
                    if layer == 0 and live(s, 1):
                        sums(s - 1, (j - 1) % UN)
                tiles(dve, step, lag=1 - layer)

            def softmax(layer):
                dve.wait_ge(s_u, (layer + 1) * T)
                dve.wait_ge(s_mul, (layer + 1) * T)
                if layer == 0:
                    dve.wait_ge(s_red, T)
                    dve.wait_ge(s_reda, T)
                dve.tensor_tensor(*(m.rearrange(f"p ({o} h) -> p c a h", c=CH, h=H) for m, o in
                                    ((BWD, "a c"), (logits, "c a"), (ulog, "c a"))), ALU.add).then_inc(s_lg, 1)
                dve.wait_ge(s_lt, layer + 1)
                link(dve.tensor_copy(LT, ps_lt))
                dve.tensor_tensor_scan(FWD, reset_f, LT, -BIG, ALU.add, ALU.max)
                dve.tensor_tensor_scan(BWD[:, ::-1], reset_b[:, ::-1], LT[:, ::-1], -BIG, ALU.add,
                                       ALU.max).then_inc(s_en, 1)
                dve.wait_ge(s_er, layer + 1)
                for i in range(2):
                    link(dve.tensor_copy(rows[:, 2 + i, :].rearrange("a (h c) -> a c h", h=H),
                                         ps[0:1, i * P:(i + 1) * P].rearrange("a (c h) -> a c h", h=H)))
                dve.tensor_tensor_scan(carry_row[:, 0, 1:P + 1], rows[:, 0, :], rows[:, 2, :], -BIG, ALU.add, ALU.max)
                link(dve.tensor_tensor_scan(carry_row[:, 1, 0:P][:, ::-1], rows[:, 1, ::-1], rows[:, 3, ::-1], -BIG,
                                            ALU.add, ALU.max))
                for i in range(2):
                    last = dve.tensor_copy(rows[:, 2 + i, :].rearrange("a (c h) -> a c h", h=H),
                                           carry_row[:, i, i:i + P].rearrange("a (h c) -> a c h", h=H))
                last.then_inc(s_cr, 1)
                dve.wait_ge(s_ca, layer + 1)
                link(dve.tensor_copy(carry[:, :], ps[:, 256:258]))
                dve.tensor_tensor_scan(FWD, reset_f, LT, carry[:, 0:1], ALU.add, ALU.max)
                link(dve.tensor_tensor_scan(BWD[:, ::-1], reset_b[:, ::-1], LT[:, ::-1], carry[:, 1:2], ALU.add,
                                            ALU.max))
                link(dve.tensor_tensor(FWD, FWD, BWD, ALU.max))
                dve.tensor_tensor(LT, LT, FWD, ALU.subtract).then_inc(s_m, 1)
                dve.wait_ge(s_et, layer + 1)
                dve.tensor_copy(logits.rearrange("p (c a h) -> p a c h", c=CH, h=H),
                                ps_lt.rearrange("p (a c h) -> p a c h", c=CH, h=H)).then_inc(s_exd, 1)
                dve.wait_ge(s_exd, layer + 1)

            def aggregate(layer):
                def step(s, j, k):
                    if live(s, 3):
                        dve.wait_ge(s_agg, layer * T + s - 2)
                    if layer == 0:
                        dve.tensor_scalar(oh_agg[j % 3], iota_t[:, 0:P], dloc[:, bass.ds(s, 1)], None,
                                          ALU.is_equal).then_inc(s_oha, 1)
                        dve.wait_ge(s_ga[j], (k + 1) * 16)
                        dve.tensor_tensor(WG[j % 3].rearrange("p (h d) -> p h d", h=H),
                                          G[j][:, 0:D].rearrange("p (h d) -> p h d", h=H),
                                          logits[:, bass.ds(s * H, H)].unsqueeze(2).to_broadcast([P, H, HD]),
                                          ALU.mult).then_inc(s_wg, 1)
                    else:
                        dve.tensor_scalar(oh_agg[j % 3], iota_t[:, 0:P], dloc[:, bass.ds(s, 1)],
                                          logits[:, bass.ds(s * H, 1)], ALU.is_equal, ALU.mult).then_inc(s_oha, 1)
                tiles(dve, step)

            def finish(layer):
                dve.wait_ge(s_agg, (layer + 1) * T)
                link(dve.tensor_scalar(rden[:, :, :].rearrange("p b h -> p (b h)"), ps[:, DEN:DEN + NB * H], 1e-30,
                                       None, ALU.max))
                link(dve.reciprocal(rden[:, :, :], rden[:, :, :]))
                for b in range(NB):
                    v, m = evac[b % 2], evac[2 + b % 2]
                    heads = H if layer == 0 else 1
                    link(dve.tensor_tensor(v.rearrange("p (h d) -> p h d", h=heads),
                                           ps[:, b * D:(b + 1) * D].rearrange("p (h d) -> p h d", h=heads),
                                           rden[:, b, 0:heads].unsqueeze(2).to_broadcast([P, heads, D // heads]),
                                           ALU.mult))
                    dve.tensor_scalar(m, v, 0.0, None, ALU.min).then_inc(s_min, 1)
                    dve.wait_ge(s_exm, layer * NB + b + 1)
                    link(dve.scalar_tensor_tensor(v, v, 0.0, m, ALU.max, ALU.add))
                    if layer == 0:
                        link(dve.scalar_tensor_tensor(h0[:, b, :], v, -1.0, h0[:, b, :], ALU.add, ALU.add))
                    else:
                        link(dve.tensor_scalar(h0[:, b, :], v, -1.0, None, ALU.add))
                for b in range(NB):
                    moments(b)
                norm(layer + 1)
                dve.wait_ge(s_lnr, (layer + 1) * 32)
                for b in range(NB):
                    dve.wait_ge(s_nrm, layer * NB + b + 1)
                    link(dve.tensor_tensor(h0[:, b, :], h0[:, b, :], lnw_row, ALU.mult))
                    if layer == 0:
                        dve.tensor_tensor(h0[:, b, :], h0[:, b, :], lnb_row, ALU.add).then_inc(s_h, 1)
                    else:
                        link(dve.tensor_tensor(h0[:, b, :], h0[:, b, :], lnb_row, ALU.add))
                        dve.wait_ge(s_x, 2 * NB * 16)
                        n = min(P, N - b * P)
                        dve.tensor_tensor(h0[0:n, b, :], h0[0:n, b, :], Wm[0:n, b, :], ALU.add).then_inc(s_res, 1)

            for layer in range(2):
                dve.wait_ge(s_fd, (layer + 1) * NB)
                if layer == 0:
                    dve.memset(logits[:, T * H:TP * H], 0.0)
                    dve.memset(ulog[:, T * H:TP * H], 0.0).then_inc(s_clear, 1)
                else:
                    dve.memset(R3[:, 0:2 * TP * H], 0.0).then_inc(s_clear, 1)
                dve.wait_ge(s_clear, layer + 1)
                scores(layer)
                softmax(layer)
                aggregate(layer)
                finish(layer)

        @block.tensor
        def _(pe):
            pe.wait_ge(s_ident, 1)
            pe.wait_ge(s_rawf, 1)
            for v in range(4):
                last = pe.transpose(ps[0:TE, v * 80:(v + 1) * 80], rawf[:, v, :], ident[0:80, 0:80])
            last.then_inc(s_cols, 1)
            pe.wait_ge(s_oh, 2)
            for t in range(TU):
                q, j = t // QJ, t % QJ
                last = pe.matmul(ps_cnt[32 * j:32 * j + 32, q * LO:(q + 1) * LO], OH[:, t, :], OL[:, t, :],
                                 start=True, stop=True)
            last.then_inc(s_cnt, 1)
            for g in range(Q // 8):
                if g:
                    pe.wait_ge(s_ohte, g)
                for q in range(8):
                    t = (g * 8 + q) * QJ
                    last = pe.transpose(ps_ohT[:, q, 0:TE], OH[:, t:t + QJ, :].rearrange("p t l -> p (t l)"),
                                        identb[0:TE, 0:TE])
                last.then_inc(s_oht, 1)
            pe.wait_ge(s_ohte, Q // 8)
            pe.wait_ge(s_lq, 1)
            pe.matmul(ps[:, 0:LO], Mhi, Lq[:, 1, :], start=True, stop=False)
            pe.matmul(ps[:, 0:LO], Mj, Lq[:, 0, :], start=False, stop=False)
            pe.matmul(ps[:, 0:LO], Mless, Tq[:, 0:1].to_broadcast([P, LO]), start=False, stop=True)
            pe.matmul(ps[:, LO:LO + NB], ones[:, :], TM[:, :], start=True, stop=True).then_inc(s_base, 1)
            for q in range(Q):
                if q % QG == 0:
                    pe.wait_ge(s_diag, q // QG + 1)
                    if q // QG >= 4:
                        pe.wait_ge(s_sel, q // QG - 3)
                at = q % (4 * QG) * P
                last = pe.matmul(ps[0:TE, at:at + P], OHT[:, q, :], diag[q], start=True, stop=True)
                if q % QG == QG - 1:
                    last.then_inc(s_look, 1)

            def project(layer):
                for i, (kind, b) in enumerate(PROJ):
                    if layer == 0 and (kind, b) in PART:
                        permute(PART[kind, b])
                    n = layer * len(PROJ) + i
                    if n >= 2:
                        pe.wait_ge(s_pe, n - 1)
                    o = slot[i % 2]
                    if kind == "T":
                        pe.wait_ge(s_h, layer * NB + b + 1)
                        for k in range(KC):
                            last = pe.transpose(o[:, k * P:(k + 1) * P], h0[:, b, k * P:(k + 1) * P], ident[:, :])
                    else:
                        pe.wait_ge(s_pe, layer * len(PROJ) + PROJ.index(("T", b)) + 1)
                        v = 2 * layer + (kind == "D")
                        for k in range(KC):
                            pe.wait_ge(s_wk[k], (v + 1) * 16)
                            for c0, c1 in ((0, 512), (512, D)):
                                last = pe.matmul(o[:, c0:c1], hT[:, k, b * P:(b + 1) * P], Wm[:, k, c0:c1],
                                                 start=k == 0, stop=k == KC - 1)
                            if b == NB - 1 and k < KC - 1:
                                last.then_inc(s_wu, 1)
                    last.then_inc(s_pp, 1)
                    if kind != "T" and b == NB - 1:
                        pe.wait_ge(s_pp, n + 1)
                        pe.sem_inc(s_wu, 1)

            def scores(layer):
                def step(s, j, k):
                    b = pe.value_load(blk[0:1, bass.ds(s, 1)], min_val=0, max_val=NB - 1)
                    if live(s, 3):
                        pe.wait_ge(s_zc, layer * T + s - 2)
                    for part in range(3):
                        for c0, c1 in ((0, 512), (512, FW)):
                            last = pe.matmul(psz[j % 3][:, c0:c1], onehotT[:, bass.ds(s * P, P)],
                                             FD[part][:, bass.ds(b * FW + c0, c1 - c0)],
                                             start=part == 0, stop=part == 2)
                    last.then_inc(s_z, 1)
                tiles(pe, step)

            def softmax(layer):
                pe.wait_ge(s_lg, layer + 1)
                for a in range(TC):
                    last = pe.transpose(ps_lt[:, a * P:(a + 1) * P], BWD[:, a * P:(a + 1) * P], ident[:, :])
                last.then_inc(s_lt, 1)
                pe.wait_ge(s_en, layer + 1)
                pe.transpose(ps[0:1, 0:P], FWD[:, L - 1:L], ident[:, :])
                pe.transpose(ps[0:1, P:2 * P], BWD[:, 0:1], ident[:, :]).then_inc(s_er, 1)
                pe.wait_ge(s_cr, layer + 1)
                pe.transpose(ps[:, 256:257], rows[:, 2, :], ident[0:1, 0:1])
                pe.transpose(ps[:, 257:258], rows[:, 3, :], ident[0:1, 0:1]).then_inc(s_ca, 1)
                pe.wait_ge(s_ex, layer + 1)
                for a in range(TC):
                    last = pe.transpose(ps_lt[:, a * P:(a + 1) * P], LT[:, a * P:(a + 1) * P], ident[:, :])
                last.then_inc(s_et, 1)

            def aggregate(layer):
                pe.wait_ge(s_exd, layer + 1)
                for b in range(8):
                    pe.matmul(ps[:, b * 512:(b + 1) * 512], zeros[:, 0:P], zeros[:, :], start=True, stop=True,
                              skip_group_check=True)

                def step(s, j, k):
                    b = pe.value_load(blk[0:1, bass.ds(s, 1)], min_val=0, max_val=NB - 1)
                    pe.wait_ge(s_oha, layer * T + s + 1)
                    if layer == 0:
                        pe.wait_ge(s_wg, s + 1)
                        rhs, den = WG[j % 3], logits[:, bass.ds(s * H, H)]
                    else:
                        pe.wait_ge(s_ga[j], (UK + k + 1) * 16)
                        rhs, den = G[j], ones[:, 0:H]
                    for c in range(D // HB):
                        pe.matmul(ps[:, bass.ds(b * D + c * HB, HB)], oh_agg[j % 3], rhs[:, c * HB:(c + 1) * HB],
                                  start=False, stop=False, skip_group_check=True)
                    pe.matmul(ps[:, bass.ds(DEN + b * H, H)], oh_agg[j % 3], den,
                              start=False, stop=False, skip_group_check=True).then_inc(s_agg, 1)
                tiles(pe, step)

            def permute(c):
                if c == 0:
                    pe.wait_ge(s_sel, Q // QG)
                    pe.matmul(ps[:, 512:1024], zeros[:, 0:P], zeros[:, :], start=True, stop=True,
                              skip_group_check=True)

                def step(t, j, k):
                    pe.wait_ge(s_scaled0, t + 1)
                    pe.wait_ge(s_scaled1, t + 1)
                    for v in range(2):
                        last = pe.matmul(ps_perm[:, v * T:(v + 1) * T], perm_l[j][1 + v], perm_r[j], start=False,
                                         stop=False, skip_group_check=True)
                    last.then_inc(s_permd, 1)
                tiles(pe, step, n=(c + 1) * PT, un=UP, first=c * PT)

            pe.wait_ge(s_sel, Q // QG - 1)
            project(0)
            pe.wait_ge(s_sorted, 1)
            pe.transpose(ps[:, 0:P], dloc[:, 0:P], ident[:, :])
            pe.transpose(ps[0:T - P, P:2 * P], dloc[:, P:T], ident[:, :]).then_inc(s_dlt, 1)
            for a in range(TC):
                last = pe.transpose(ps_lt[:, a * P:(a + 1) * P], BWD[:, a * P:(a + 1) * P], ident[:, :])
            last.then_inc(s_vt, 1)
            pe.wait_ge(s_vs, 1)
            pe.matmul(ps[:, 256:257], shift_up[:, :], LT[:, L - 1:L], start=True, stop=True)
            pe.matmul(ps[:, 257:258], shift_dn[:, :], LT[:, 0:1], start=True, stop=True).then_inc(s_vse, 1)
            pe.wait_ge(s_dlte, 2)
            pe.wait_ge(s_vs, 2)
            pe.transpose(ps[0:1, 0:P], ends[:, 0:1], ident[:, :])
            pe.transpose(ps[0:1, P:2 * P], ends[:, 1:2], ident[:, :]).then_inc(s_vse, 1)
            pe.wait_ge(s_edges, 1)
            for layer in range(2):
                if layer:
                    project(1)
                pe.wait_ge(s_fd, (layer + 1) * NB)
                scores(layer)
                softmax(layer)
                aggregate(layer)


INS = ["x", "src", "dst", "L0_gnn_W1s", "L0_gnn_b1s", "L0_gnn_W1d", "L0_gnn_b1d", "L0_gnn_attn1",
       "L0_gnn_ln1_w", "L0_gnn_ln1_b", "L0_gnn_Wos", "L0_gnn_bos", "L0_gnn_Wod", "L0_gnn_bod",
       "L0_gnn_attno", "L0_gnn_lno_w", "L0_gnn_lno_b"]


def kernel(**inputs):
    import numpy as np
    import concourse.bacc as bacc
    from concourse.bass_utils import run_bass_kernel_spmd

    nc = bacc.Bacc("TRN2", target_bir_lowering=False, num_devices=1)
    arrays, args = {}, []
    for name in INS:
        a = np.ascontiguousarray(inputs[name])
        arrays[f"in_{name}"] = a
        args.append(nc.dram_tensor(f"in_{name}", a.shape, mybir.dt.from_np(a.dtype), kind="ExternalInput").ap())
    args.append(nc.dram_tensor("out_0", (N, D), f32, kind="ExternalOutput").ap())
    gnn_program(nc, *args)
    r = run_bass_kernel_spmd(nc, [arrays], core_ids=[0])
    return r.results[0]["out_0"]
```

```python
import concourse.bass as bass
from concourse import mybir
from contextlib import ExitStack


P = 128
N = 625
NB = 5
NP = NB * P
D = 768
H = 8
HD = D // H
KC = D // P
E = 20000
TE = 125
TU = E // TE
QJ = 4
Q = TU // QJ
LO = 32
UN = 9
PARTS = 3
GI = 2
TURNS = 2
UI = TURNS * UN
HA = 2
LU = 6
LG = 3
T = 162
assert T * P >= E + NB * (P - 1) and T % UI == 0
UK = T // UN
CH = 16
TC = 11
TP = CH * TC
L = TC * P
FW = D + H
EPS = 1e-5
SLOPE = 0.2
BIG = 1e30
BANK = 512
PIECES = [(0, 512, 0, BANK), (512, 682, 5 * BANK, 171), (682, FW, 7 * BANK, FW - 682)]
SPAN = [(0, 512, 0, BANK), (512, NP, 5 * BANK, P)]
for c0, c1, at, step in PIECES + SPAN:
    assert all((at + b * step) // BANK == (at + b * step + c1 - c0 - 1) // BANK for b in range(NB))
CHUNK = 4
CE = E // CHUNK
CTU = TU // CHUNK
UR = 20
UE = 4
UP = 8
PT = TU // NB
QG = 8

f32 = mybir.dt.float32
bf16 = mybir.dt.bfloat16
f16 = mybir.dt.float16
i32 = mybir.dt.int32
ALU = mybir.AluOpType
ACT = mybir.ActivationFunctionType
AX = mybir.AxisListType


PROJ = [("T", 0), ("T", 1), ("D", 0), ("T", 2), ("D", 1), ("T", 3), ("D", 2), ("T", 4),
        ("D", 3), ("D", 4), ("F", 0), ("F", 1), ("F", 2), ("F", 3), ("F", 4)]
PART = {("F", 0): 0, ("F", 1): 1, ("F", 2): 2, ("F", 3): 3, ("F", 4): 4}


def live(s, back, n=T):
    return not isinstance(s, int) or 0 <= s - back < n


def tiles(eng, body, lag=0, n=T, un=UN, turns=1, first=0):
    w = un * turns
    if first == 0:
        for s in range(w):
            body(s, s % un, s // un)
    with eng.Fori(max(first // w, 1), n // w) as i:
        for j in range(w):
            body(i * w + j, j % un, i * turns + j // un)
    for s in range(n, n + lag):
        body(s, s % un, s // un)


def gnn_program(nc, x, src, dst, W1s, b1s, W1d, b1d, attn1, ln1_w, ln1_b,
                Wos, bos, Wod, bod, attno, lno_w, lno_b, out):
    ctx = ExitStack()
    with ctx:
        def sb(name, shape, dt):
            return ctx.enter_context(nc.sbuf_tensor(name, shape, dt))

        def sem(name):
            return ctx.enter_context(nc.semaphore(name))

        tables = [nc.dram_tensor(f"fs_table{l}", (NP, FW), f32, kind="Internal").ap() for l in range(2)]
        dl_rows = nc.dram_tensor("dl_rows", (T, P), bf16, kind="Internal").ap()

        R1 = sb("R1", [P, T * P // 2], f32)
        onehotT = R1[:, :].bitcast(bf16)
        dst_row = [R1[0:TE, c * CE:(c + 1) * CE].bitcast(i32) for c in range(2)]
        GW, YW = UN * FW, 3 * FW + 3 * P
        R2W = max(GW + YW + 2 * L, TU * LO + Q * TE + 2 * Q * LO)
        R2 = sb("R2", [P, R2W], f32)
        G = [R2[:, i * FW:(i + 1) * FW] for i in range(UN)]
        Y = [R2[:, GW + i * D:GW + (i + 1) * D] for i in range(3)]
        WG = [R2[:, GW + i * FW:GW + (i + 1) * FW] for i in range(3)]
        oh_agg = [R2[:, GW + 3 * FW + i * P:GW + 3 * FW + (i + 1) * P] for i in range(3)]
        reset_f = R2[:, R2W - 2 * L:R2W - L]
        reset_b = R2[:, R2W - L:R2W]
        LT, FWD, BWD = (R2[:, i * L:(i + 1) * L] for i in range(3))
        assert 3 * L <= GW
        agg_v = [R2[:, i * D:(i + 1) * D] for i in range(NB)]
        agg_e = [R2[:, (NB + i) * D:(NB + 1 + i) * D] for i in range(3)]
        lnw_row, lnb_row = (R2[:, (NB + 3 + i) * D:(NB + 4 + i) * D] for i in range(2))
        Wn = R2[:, 0:KC * D].rearrange("p (k n) -> p k n", k=KC)
        assert (NB + 5) * D <= R2W - 2 * L
        at = GW
        oh_src = [R2[:, at + i * NP // 2:at + (i + 1) * NP // 2].bitcast(bf16) for i in range(3)]
        at += 3 * NP // 2
        oh_ex = [R2[:, at + i * 3 * P // 2:at + (i + 1) * 3 * P // 2].bitcast(bf16).rearrange("p (v n) -> p v n", v=3)
                 for i in range(3)]
        at += 9 * P // 2
        ex_part = R2[:, at:at + 3 * T].rearrange("p (v t) -> p v t", v=3)
        ex_cast = R2[:, at + 3 * T:at + 3 * T + T // 2].bitcast(bf16)
        assert at + 3 * T + T // 2 <= GW + YW
        oh_dst = [R2[:, 3 * L + i * P // 2:3 * L + (i + 1) * P // 2].bitcast(bf16) for i in range(3)]
        FS = R1[:, 0:NB * D].rearrange("p (b n) -> p b n", b=NB)
        dense = R1[:, NB * D:NB * D + NB * NP].rearrange("p (b n) -> p b n", b=NB)
        iota_s = R1[:, NB * (D + NP):NB * (D + NP) + NP // 2].bitcast(f16)
        src_col = R1[:, NB * (D + NP) + NP // 2:NB * (D + NP) + NP // 2 + T]
        assert NB * (D + NP) + NP // 2 + T <= T * P // 2
        OH = R2[0:TE, 0:TU * LO // 2].bitcast(bf16).rearrange("p (t l) -> p t l", l=LO)
        OL = R2[0:TE, TU * LO // 2:TU * LO].bitcast(bf16).rearrange("p (t l) -> p t l", l=LO)
        OHT = R2[:, TU * LO:TU * LO + Q * TE].rearrange("p (q e) -> p q e", e=TE)
        raw = R2[0:80, TU * LO:TU * LO + 4 * TE].bitcast(i32).rearrange("q (v p) -> q v p", p=TE)
        rawf = R2[0:80, TU * LO + 4 * TE:TU * LO + 8 * TE].rearrange("q (v p) -> q v p", p=TE)
        CT = R2[:, TU * LO + Q * TE:TU * LO + Q * TE + Q * LO]
        TAB = R2[:, TU * LO + Q * TE + Q * LO:TU * LO + Q * TE + 2 * Q * LO]
        sel = R2[0:TE, 0:QG * P]
        assert QJ * LO == P and 2 * QG * P <= TU * LO // 2 and QG <= LO * Q // P
        diag = [R2[:, at:at + QG * P].rearrange("p (q c) -> p q c", c=P)
                for at in (QG * P, TU * LO + Q * TE)]
        perm_l = [[R2[0:TE, i * P // 2:(i + 1) * P // 2].bitcast(f16) for i in range(u, u + 3)]
                  for u in range(0, 3 * UP, 3)]
        at = 3 * UP * P // 2
        perm_r = [R2[0:TE, at + i * T // 2:at + (i + 1) * T // 2].bitcast(f16) for i in range(UP)]
        assert at + UP * T // 2 <= TU * LO // 2

        h0 = sb("h0", [P, NB, D], f32)
        R3 = sb("R3", [P, KC * NP], f32)
        hT = R3[:, :].rearrange("p (k n) -> p k n", k=KC)
        logits = R3[:, 0:TP * H]
        ulog = R3[:, TP * H:2 * TP * H]
        denseT = R3[:, 0:NB * NP].rearrange("p (i n) -> p i n", n=P)
        assert 2 * TP * H <= KC * NP and NB * NP <= KC * NP
        Wm = sb("Wm", [P, KC, D], f32)
        bias = [sb(f"bias{i}", [P, D], f32) for i in range(2)]
        attn_row = sb("attn_row", [P, D], f32)
        FD = [sb(f"FD{i}", [P, NB * FW], bf16) for i in range(3)]
        ftile = [sb(f"ftile{i}", [P, FW], f32) for i in range(2)]
        utmp = sb("utmp", [P, D], f32)

        ident = sb("ident", [P, P], f32)
        identb = sb("identb", [P, P], bf16)
        diff = sb("diff", [P, P], f32)
        ltmask = sb("ltmask", [P, P], f32)
        shift_up = sb("shift_up", [P, P], f32)
        shift_dn = sb("shift_dn", [P, P], f32)
        iota_t = sb("iota_t", [P, T + UN], f32)
        iota_h = sb("iota_h", [P, T + UN], f16)
        iota_p = sb("iota_p", [P, 1], f32)
        zeros = sb("zeros", [P, 512], bf16)
        zerof = sb("zerof", [P, LO], f32)
        ones = sb("ones", [P, P], f32)
        ci = sb("ci", [P, 4, P], i32)
        pi = sb("pi", [P, 4], i32)
        pf = sb("pf", [P, 4], f32)
        M = sb("M", [P, 5, P], f32)
        Mhi, Mj, Mless, Msame, Mgroup = (M[:, i, :] for i in range(5))
        bm5 = sb("bm5", [P, NB], f32)
        lm5 = sb("lm5", [P, NB], f32)
        dcol = sb("dcol", [TE, TU], f32)
        dcol1 = sb("dcol1", [TE, TU], f32)
        scol = sb("scol", [TE, TU], f32)
        dint = sb("dint", [TE, 3, TU], i32)
        hif = sb("hif", [TE, 2, TU], f32)
        pos = sb("pos", [TE, TU], f32)
        rank = sb("rank", [TE, TU], f32)
        eqj = sb("eqj", [TE, UE, TE], bf16)
        Lq = sb("Lq", [P, 3, LO], f32)
        Tq = sb("Tq", [P, 1], f32)
        TM = sb("TM", [P, NB], f32)
        nt = sb("nt", [P, 4, NB], f32)
        nti = sb("nti", [P, 2, NB], i32)
        start = sb("start", [P, 1], f32)
        base2 = sb("base2", [P, LO], f32)
        blkf = sb("blkf", [1, 2, T + UN], f32)
        blk = sb("blk", [1, T + UN], i32)
        packed = sb("packed", [1, UK], i32)
        srcs = sb("srcs", [P, T + UN], i32)
        vcol = sb("vcol", [P, TP], f32)
        dloc_i = sb("dloc_i", [P, 2, T], i32)
        dloc = sb("dloc", [P, T], f32)
        dlT = sb("dlT", [P, 2, P], bf16)
        head_sums = sb("head_sums", [P, UI, H - HA], f32)
        edge_ix = sb("edge_ix", [P, UI], i32)
        ends = sb("ends", [P, 4], f32)
        rows = sb("rows", [1, 4, P], f32)
        carry_row = sb("carry_row", [1, 2, P + 1], f32)
        carry = sb("carry", [P, 2], f32)
        row_sum = sb("row_sum", [P, NB, 2], f32)
        stats = sb("stats", [P, NB, 2, 6], f32)
        mv = sb("mv", [P, NB, 2], f32)
        std = sb("std", [P, NB], f32)
        rstd = sb("rstd", [P, NB], f32)
        nmr = sb("nmr", [P, NB], f32)
        rden = sb("rden", [P, NB, H], f32)

        ps = ctx.enter_context(nc.psum_tensor("ps", [P, 4096], f32))
        slot = [ps[:, 2048:2048 + D], ps[:, 3072:3072 + D]]
        psz = [ps[:, i * 1024:i * 1024 + FW] for i in range(3)]
        prod = [ps[:, i * 1024:i * 1024 + D] for i in range(4)]
        ps_cnt = ps[:, 512:512 + Q * LO]
        ps_ohT = ps[:, 0:512].bitcast(bf16).rearrange("p (q e) -> p q e", e=P)
        ps_perm = ps[:, 512:512 + 2 * T]
        ps_lt = ps[:, 512:512 + L]

        s_load = sem("s_load")
        s_x = sem("s_x")
        s_wk = [sem(f"s_wk{k}") for k in range(KC)]
        s_wu = sem("s_wu")
        s_rows = sem("s_rows")
        s_attn = sem("s_attn")
        s_drow = [sem("s_drow0"), sem("s_drow1")]
        s_const = sem("s_const")
        s_dve = sem("s_dve")
        s_ident = sem("s_ident")
        s_rawf = sem("s_rawf")
        s_cols = sem("s_cols")
        s_oh = sem("s_oh")
        s_cnt = sem("s_cnt")
        s_oht = sem("s_oht")
        s_ohte = sem("s_ohte")
        s_lq = sem("s_lq")
        s_base = sem("s_base")
        s_look = sem("s_look")
        s_sel = sem("s_sel")
        s_rank = sem("s_rank")
        s_diag = sem("s_diag")
        s_perm = sem("s_perm")
        s_scaled0 = sem("s_scaled0")
        s_scaled1 = sem("s_scaled1")
        s_permd = sem("s_permd")
        s_zero = sem("s_zero")
        s_sorted = sem("s_sorted")
        s_dlt = sem("s_dlt")
        s_dlte = sem("s_dlte")
        s_dlw = sem("s_dlw")
        s_dlb = [sem(f"s_dlb{c}") for c in range(PARTS)]
        s_ohT = sem("s_ohT")
        s_vt = sem("s_vt")
        s_vs = sem("s_vs")
        s_vse = sem("s_vse")
        s_edges = sem("s_edges")
        s_h = sem("s_h")
        s_pp = sem("s_pp")
        s_pe = sem("s_pe")
        s_fb = sem("s_fb")
        s_um = sem("s_um")
        s_fu = sem("s_fu")
        s_tw = [sem("s_tw0"), sem("s_tw1")]
        s_hi = sem("s_hi")
        s_r1 = sem("s_r1")
        s_mid = sem("s_mid")
        s_fd = sem("s_fd")
        s_clear = sem("s_clear")
        s_ix = sem("s_ix")
        s_gs = [sem(f"s_gs{i}") for i in range(UN)]
        s_ga = [sem(f"s_ga{i}") for i in range(UN)]
        s_z = sem("s_z")
        s_zc = sem("s_zc")
        s_u = sem("s_u")
        s_mul = sem("s_mul")
        s_yact = sem("s_yact")
        s_kept = sem("s_kept")
        s_reda = sem("s_reda")
        s_lg = sem("s_lg")
        s_lt = sem("s_lt")
        s_en = sem("s_en")
        s_er = sem("s_er")
        s_cr = sem("s_cr")
        s_ca = sem("s_ca")
        s_m = sem("s_m")
        s_ex = sem("s_ex")
        s_et = sem("s_et")
        s_exd = sem("s_exd")
        s_oha = sem("s_oha")
        s_wg = sem("s_wg")
        s_wd = sem("s_wd")
        s_sum = sem("s_sum")
        s_agg = sem("s_agg")
        s_lnr = sem("s_lnr")
        s_rden = sem("s_rden")
        s_less = sem("s_less")
        s_div = sem("s_div")
        s_exp = sem("s_exp")
        s_relu = sem("s_relu")
        s_radd = sem("s_radd")
        s_elu = sem("s_elu")
        s_var = sem("s_var")
        s_std = sem("s_std")
        s_ln = sem("s_ln")
        s_nrm = sem("s_nrm")
        s_fs = sem("s_fs")
        s_col = sem("s_col")
        s_ohd = sem("s_ohd")
        s_ohx1 = sem("s_ohx1")
        s_ohx2 = sem("s_ohx2")
        s_ohs = sem("s_ohs")
        s_part = sem("s_part")
        s_dense = sem("s_dense")
        s_tr = sem("s_tr")
        s_tre = sem("s_tre")
        s_prod = sem("s_prod")
        s_xb = sem("s_xb")
        s_res = sem("s_res")
        s_out = sem("s_out")

        block = ctx.enter_context(nc.Block())
        attn_in = [attn1.rearrange("h d -> (h d)"), attno.rearrange("h d -> (h d)")]
        bvec = [[b1d, b1s], [bod, bos]]
        wmat = [[W1d, W1s], [Wod, Wos]]
        lnv = [(ln1_w, ln1_b), (lno_w, lno_b)]

        def row(v):
            return v.rearrange("(a n) -> a n", a=1)

        @block.sync
        def _(sp):
            for v, e in enumerate((dst, src)):
                sp.dma_start(raw[:, 2 * v:2 * v + 2, :], e.rearrange("(a q p) -> q a p", a=2, p=TE)
                             ).then_inc(s_load, 16)

            def drow(c):
                sp.dma_start(dst_row[c % 2], row(dst)[:, c * CE:(c + 1) * CE].partition_broadcast(TE)
                             ).then_inc(s_drow[c % 2], 16)

            drow(0)
            for b in range(NB):
                n = min(P, N - b * P)
                if n < P:
                    sp.wait_ge(s_zero, 1)
                sp.dma_start(h0[0:n, b, :], x[b * P:b * P + n, :]).then_inc(s_x, 16)
            drow(1)
            for c in range(2, CHUNK):
                sp.wait_ge(s_rank, (c - 1) * CTU)
                drow(c)

            def table_out(layer):
                for b in range(NB):
                    u = NB + b
                    sp.wait_ge(s_fu, layer * 2 * NB + u + 1)
                    sp.dma_start(tables[layer][b * P:(b + 1) * P, :], ftile[u % 2][:, :]).then_inc(s_tw[u % 2], 16)

            table_out(0)
            sp.wait_ge(s_dlte, 2)
            sp.dma_start(dl_rows[0:P, :], dlT[:, 0, :]).then_inc(s_dlw, 16)
            sp.dma_start(dl_rows[P:T, :], dlT[0:T - P, 1, :]).then_inc(s_dlw, 16)
            sp.wait_ge(s_dlw, 32)
            for c in range(PARTS):
                w = T * P // PARTS
                sp.dma_start(onehotT[:, c * w:(c + 1) * w], dl_rows.rearrange("(a t) p -> a (t p)", a=1)[
                    :, c * w:(c + 1) * w].partition_broadcast(P)).then_inc(s_dlb[c], 16)
            table_out(1)
            sp.wait_ge(s_z, 2 * T)
            sp.wait_ge(s_tw[0], 64)
            sp.wait_ge(s_tw[1], 96)
            for b in range(NB):
                sp.dma_start(FS[:, b, :], tables[1][b * P:(b + 1) * P, 0:D]).then_inc(s_fs, 16)
            sp.wait_ge(s_pp, 2 * len(PROJ))
            for b in range(NB):
                n = min(P, N - b * P)
                sp.dma_start(Wm[0:n, b, :], x[b * P:b * P + n, :]).then_inc(s_x, 16)
            for b in range(NB):
                n = min(P, N - b * P)
                sp.wait_ge(s_res, b + 1)
                sp.dma_start(out[b * P:b * P + n, :], h0[0:n, b, :]).then_inc(s_out, 16)
            sp.wait_ge(s_out, NB * 16)

        @block.gpsimd
        def _(pool):
            def iota(o, pattern, base, mult):
                pool.iota(o, pattern, base=base, channel_multiplier=mult,
                          allow_small_or_imprecise_dtypes=True).then_inc(s_const, 1)
            iota(diff[:, :], [[1, P]], 0, -1)
            iota(iota_t[:, :], [[1, T + UN]], 0, 0)
            iota(iota_p[:, :], [[0, 1]], 0, 1)
            iota(ci[:, 0, :], [[1, P]], 0, 0)
            iota(pi[:, 0:1], [[0, 1]], 0, 1)
            pool.memset(h0[:, NB - 1, :], 0.0).then_inc(s_zero, 1)

            def permute(c):
                def step(t, j, k):
                    pool.wait_ge(s_perm, t + 1)
                    if live(t, UP, TU):
                        pool.wait_ge(s_permd, t - UP + 1)
                    pool.tensor_tensor(perm_l[j][2], perm_l[j][0], dcol1[:, bass.ds(t, 1)].to_broadcast([TE, P]),
                                       ALU.mult).then_inc(s_scaled1, 1)
                tiles(pool, step, n=(c + 1) * PT, un=UP, first=c * PT, turns=TURNS)

            def project(layer):
                parts = [[PART[PROJ[i + 1]] for i in range(PROJ.index(("DF"[u // NB], u % NB)) + 1)
                          if i + 1 < len(PROJ) and PROJ[i + 1] in PART
                          and (u == 0 or i > PROJ.index(("DF"[(u - 1) // NB], (u - 1) % NB)))]
                         for u in range(2 * NB)]
                if layer == 0:
                    pool.wait_ge(s_rows, 48)
                    pool.wait_ge(s_attn, 1)
                for u in range(NB if layer else 2 * NB):
                    n, f, b = layer * 2 * NB + u, ftile[u % 2], u % NB
                    i = PROJ.index(("DF"[u // NB], b))
                    if layer == 0:
                        for part in parts[u]:
                            permute(part)
                        pool.wait_ge(s_pe, i + 1)
                        pool.tensor_tensor(f[:, 0:D], f[:, 0:D], bias[u // NB][:, :], ALU.add).then_inc(s_fb, 1)
                        pool.wait_ge(s_fb, n + 1)
                        if n:
                            pool.wait_ge(s_fu, n)
                        pool.tensor_tensor(utmp[:, :], f[:, 0:D], attn_row[:, :], ALU.mult).then_inc(s_um, 1)
                    if u < NB:
                        m, o = layer * NB + b + 1, b * FW
                        pool.wait_ge(s_hi, m)
                        pool.tensor_tensor(f[:, :], f[:, :], FD[0][:, o:o + FW], ALU.subtract).then_inc(s_r1, 1)
                        pool.wait_ge(s_mid, m)
                        pool.tensor_tensor(FD[2][:, o:o + FW], f[:, :], FD[1][:, o:o + FW],
                                           ALU.subtract).then_inc(s_fd, 1)

            def gather(layer, phase):
                turn = 2 * layer + phase
                used, before = (s_wg, 0) if layer == 0 else (s_agg, T)
                if turn:
                    pool.wait_ge(s_ix, turn * (T // GI + 1))
                pool.tensor_copy(edge_ix[:, 0:GI], srcs[:, 0:GI]).then_inc(s_ix, 1)

                def step(s, j, k):
                    if j % GI == 0:
                        pool.wait_ge(s_ix, turn * (T // GI + 1) + k * (UI // GI) + j // GI + 1)
                        if phase == 0:
                            pool.wait_ge(s_zc, layer * T + s + GI)
                        elif live(s + GI - 1, UN):
                            pool.wait_ge(used, before + s + GI - UN)
                        at = (j + GI) % UI
                        pool.tensor_copy(edge_ix[:, at:at + GI], srcs[:, bass.ds(s + GI, GI)]).then_inc(s_ix, 1)
                    pool.indirect_dma_start(G[j % UN], None, tables[layer],
                                            bass.IndirectOffsetOnAxis(ap=edge_ix[:, j:j + 1], axis=0),
                                            compute_op=(ALU.add, ALU.bypass)[phase]
                                            ).then_inc((s_gs, s_ga)[phase][j % UN], 16)
                tiles(pool, step, un=UI)

            for layer in range(2):
                project(layer)
                if layer == 0:
                    pool.wait_ge(s_edges, 1)
                else:
                    pool.wait_ge(s_ln, 2)
                pool.wait_ge(s_tw[0], (layer + 1) * 32)
                pool.wait_ge(s_tw[1], (layer + 1) * 48)
                gather(layer, 0)
                if layer == 0:
                    pool.wait_ge(s_exd, 1)
                    gather(0, 1)
                    pool.wait_ge(s_less, 1)
                    for b in range(NB):
                        pool.wait_ge(s_relu, b + 1)
                        pool.tensor_tensor(h0[:, b, :], h0[:, b, :], agg_v[b], ALU.add).then_inc(s_radd, 1)
                else:
                    pool.wait_ge(s_z, 2 * T)
                    pool.iota(iota_s, [[1, NP]], base=0, channel_multiplier=0,
                              allow_small_or_imprecise_dtypes=True).then_inc(s_col, 1)
                    pool.wait_ge(s_part, 1)

                    def times_ex(s, j, k):
                        pool.wait_ge(s_ohd, s + 1)
                        if live(s, 3):
                            pool.wait_ge(s_agg, T + s - 2)
                        pool.tensor_tensor(oh_ex[j % 3][:, 2, :], oh_dst[j % 3],
                                           ex_part[:, 2, bass.ds(s, 1)].to_broadcast([P, P]),
                                           ALU.mult).then_inc(s_ohx2, 1)
                    tiles(pool, times_ex, turns=TURNS)
                    pool.wait_ge(s_x, 2 * NB * 16)
                    pool.wait_ge(s_lnr, 64)
                    for b in range(NB):
                        n = min(P, N - b * P)
                        pool.tensor_tensor(Wm[0:n, b, :], Wm[0:n, b, :], lnb_row[0:n, :], ALU.add).then_inc(s_xb, 1)

        @block.scalar
        def _(act):
            def weights(layer):
                for i in range(2):
                    for k in range(KC):
                        if i and layer == 0:
                            act.wait_ge(s_wu, k + 1)
                        act.dma_start((Wn if i and layer else Wm)[:, k, :],
                                      wmat[layer][i][k * P:(k + 1) * P, :]).then_inc(s_wk[k], 16)
                    yield

            def small_rows(layer):
                for i in range(2):
                    act.dma_start(bias[i][:, :], row(bvec[layer][i]).partition_broadcast(P)).then_inc(s_rows, 16)
                act.dma_start(attn_row[:, :], row(attn_in[layer]).partition_broadcast(P)).then_inc(s_rows, 16)
                act.wait_ge(s_rows, (layer + 1) * 48)
                act.activation(attn_row[:, :], attn_row[:, :], ACT.Copy, scale=1.0 - SLOPE).then_inc(s_attn, 1)

            def project(layer, loads):
                def post(u):
                    n, f, b = layer * 2 * NB + u, ftile[u % 2], u % NB
                    act.wait_ge(s_um, n + 1)
                    if layer == 0:
                        for h in range(H):
                            v = utmp[:, h * HD:(h + 1) * HD]
                            last = act.activation(v, v, ACT.Copy, scale=SLOPE / (1.0 - SLOPE),
                                                  accum_out=f[:, D + h:D + h + 1])
                    else:
                        last = act.activation(f[:, D + 1:FW], zerof[:, 1:H], ACT.Copy)
                    last.then_inc(s_fu, 1)
                    if u < NB:
                        o = b * FW
                        act.wait_ge(s_fu, n + 1)
                        act.activation(FD[0][:, o:o + FW], f[:, :], ACT.Copy).then_inc(s_hi, 1)
                        act.wait_ge(s_r1, layer * NB + b + 1)
                        act.activation(FD[1][:, o:o + FW], f[:, :], ACT.Copy).then_inc(s_mid, 1)

                u, waiting = 0, None
                for i, (kind, b) in enumerate(PROJ):
                    if layer == 0 and i + 1 < len(PROJ) and PROJ[i + 1] in PART:
                        if waiting is not None:
                            post(waiting)
                            waiting = None
                        permute(PART[PROJ[i + 1]])
                    act.wait_ge(s_pp, layer * len(PROJ) + i + 1)
                    if kind == "T":
                        act.activation(hT[:, :, b * P:(b + 1) * P], slot[i % 2].rearrange("p (k n) -> p k n", n=P),
                                       ACT.Copy).then_inc(s_pe, 1)
                        continue
                    if 2 <= u < NB + 2:
                        act.wait_ge(s_fd, layer * NB + u - 2 + 1)
                    elif u >= NB + 2:
                        act.wait_ge(s_tw[u % 2], (layer * (2 + u % 2) + (u - 2 - NB) // 2 + 1) * 16)
                    act.activation(ftile[u % 2][:, 0:D], slot[i % 2], ACT.Copy).then_inc(s_pe, 1)
                    if waiting is not None:
                        post(waiting)
                    waiting = u
                    u += 1
                    if u == NB and layer == 0:
                        next(loads)
                post(waiting)

            def permute(c):
                def step(t, j, k):
                    act.wait_ge(s_perm, t + 1)
                    if live(t, UP, TU):
                        act.wait_ge(s_permd, t - UP + 1)
                    act.activation(perm_l[j][1], perm_l[j][0], ACT.Copy,
                                   scale=scol[:, bass.ds(t, 1)]).then_inc(s_scaled0, 1)
                tiles(act, step, n=(c + 1) * PT, un=UP, first=c * PT, turns=TURNS)

            def scores(layer):
                def copy(s, j):
                    act.wait_ge(s_z, layer * T + s + 1)
                    if live(s, UN):
                        act.wait_ge(s_mul, layer * T + s - UN + 1)
                        act.wait_ge(s_u, layer * T + s - UN + 1)
                    act.activation(G[j], psz[j % 3], ACT.Copy).then_inc(s_zc, 1)

                def linear(s, j, k):
                    for i in range(j - LG + 1, j + 1):
                        act.wait_ge(s_gs[i], (layer * (T // UN) + k + 1) * 16)
                    rows = R2[:, (j - LG + 1) * FW:(j + 1) * FW].rearrange("p (t c) -> p t c", c=FW)
                    act.activation(ulog[:, bass.ds((s - LG + 1) * H, LG * H)].rearrange("p (t h) -> p t h", h=H),
                                   rows[:, :, D:FW], ACT.Copy).then_inc(s_u, LG)

                def heads(s, j):
                    act.wait_ge(s_yact, s + 1)
                    for h in range(H - HA, H):
                        y = Y[j % 3][:, h * HD:(h + 1) * HD]
                        last = act.activation(y, y, ACT.Copy, accum_out=logits[:, bass.ds(s * H + h, 1)])
                    last.then_inc(s_reda, 1)

                def step(s, j, k):
                    if live(s, 0):
                        copy(s, j)
                    if isinstance(s, int) and s == LU:
                        act.wait_ge(s_clear, layer + 1)
                    if live(s, LU) and (j - LU) % UN % LG == LG - 1:
                        linear(s - LU, (j - LU) % UN, k - (j < LU))
                    if layer == 0 and live(s, LU + 1):
                        heads(s - LU - 1, (j - LU - 1) % UN)
                tiles(act, step, lag=LU + 1, turns=TURNS)

            def std_of(n, blocks=slice(0, NB)):
                act.wait_ge(s_var, n + 1)
                act.activation(std[:, blocks], std[:, blocks], ACT.Sqrt).then_inc(s_std, 1)
                act.wait_ge(s_ln, n + 1)

            def normalise(blocks):
                for b in blocks:
                    act.activation(h0[:, b, :], h0[:, b, :], ACT.Identity, bias=nmr[:, b:b + 1],
                                   scale=rstd[:, b:b + 1]).then_inc(s_nrm, 1)

            loads = weights(0)
            next(loads)
            small_rows(0)
            for g in range(Q // 8):
                act.wait_ge(s_oht, g + 1)
                act.activation(OHT[:, g * 8:(g + 1) * 8, :], ps_ohT[:, :, 0:TE], ACT.Copy).then_inc(s_ohte, 1)
            std_of(0)
            for b in range(NB):
                act.activation(h0[:, b, :], h0[:, b, :], ACT.Relu, bias=nmr[:, b:b + 1],
                               scale=rstd[:, b:b + 1]).then_inc(s_h, 1)
            for layer in range(2):
                project(layer, loads)
                scores(layer)
                if layer == 0:
                    loads = weights(1)
                    next(loads)
                    act.wait_ge(s_mul, T)
                    small_rows(1)
                    act.activation(h0[:, :, :], h0[:, :, :], ACT.Copy, bias=-1.0).then_inc(s_less, 1)
                act.wait_ge(s_m, layer + 1)
                act.activation(LT, LT, ACT.Exp).then_inc(s_ex, 1)
                if layer == 0:
                    def beside(s, j, k):
                        if live(s, 3):
                            act.wait_ge(s_agg, s - 2)
                        act.activation(WG[j % 3][:, D:FW], logits[:, bass.ds(s * H, H)], ACT.Copy).then_inc(s_wd, 1)
                    act.wait_ge(s_exd, 1)
                    tiles(act, beside, turns=TURNS)
                else:
                    def times_ex(s, j, k):
                        act.wait_ge(s_ohd, s + 1)
                        if live(s, 3):
                            act.wait_ge(s_agg, T + s - 2)
                        act.activation(oh_ex[j % 3][:, 1, :], oh_dst[j % 3], ACT.Copy,
                                       scale=ex_part[:, 1, bass.ds(s, 1)]).then_inc(s_ohx1, 1)
                    act.wait_ge(s_part, 1)
                    tiles(act, times_ex, turns=TURNS)
                act.wait_ge(s_agg, (layer + 1) * T)
                for v, r in zip(lnv[layer], (lnw_row, lnb_row)):
                    act.dma_start(r, row(v).partition_broadcast(P)).then_inc(s_lnr, 16)
                if layer:
                    for b in range(NB):
                        for i, (c0, c1, at, step) in enumerate(SPAN):
                            last = act.activation(dense[:, b, c0:c1], ps[:, at + b * step:at + b * step + c1 - c0],
                                                  ACT.Copy, accum_out=row_sum[:, b, i:i + 1])
                        last.then_inc(s_dense, 1)
                    for i in range(0, NB * NB, 4):
                        n = min(4, NB * NB - i)
                        act.wait_ge(s_tr, i // 4 + 1)
                        act.activation(denseT[:, i:i + n, :], ps[:, i * P:(i + n) * P].rearrange(
                            "p (i n) -> p i n", n=P), ACT.Copy).then_inc(s_tre, 1)
                if layer:
                    act.wait_ge(s_rden, 2)

                def sums(b):
                    for c0, c1, at, step in PIECES:
                        if b == 0 and c1 == FW:
                            act.wait_ge(s_rden, 1)
                        last = act.activation(agg_v[b][:, c0:min(c1, D)],
                                              ps[:, at + b * step:at + b * step + min(c1, D) - c0], ACT.Copy)
                    last.then_inc(s_sum, 1)

                if layer == 0:
                    for b in range(3):
                        sums(b)
                    for b in range(NB):
                        v = agg_v[b]
                        act.wait_ge(s_div, b + 1)
                        if b >= 3:
                            act.wait_ge(s_elu, b - 2)
                        act.activation(agg_e[b % 3], v, ACT.Exp).then_inc(s_exp, 1)
                        act.wait_ge(s_exp, b + 1)
                        act.activation(v, v, ACT.Relu).then_inc(s_relu, 1)
                        if b + 3 < NB:
                            sums(b + 3)
                else:
                    for n, blocks in ((2, range(NB - 1)), (3, range(NB - 1, NB))):
                        for b in blocks:
                            if b >= 3:
                                act.wait_ge(s_elu, NB + b - 2)
                            act.wait_ge(s_prod, b + 1)
                            for o, fn in ((agg_v[b], ACT.Relu), (agg_e[b % 3], ACT.Exp)):
                                last = act.activation(o, prod[b % 4], fn, scale=rden[:, b, 0:1])
                            last.then_inc(s_sum, 1)
                        std_of(n, slice(blocks[0], blocks[-1] + 1))
                        normalise(blocks)
                if layer == 0:
                    std_of(1)
                    normalise(range(NB))
                    next(loads)

        @block.vector
        def _(dve):
            own = [0]

            def link(ins):
                own[0] += 1
                ins.then_inc(s_dve, 1)
                dve.wait_ge(s_dve, own[0])

            def moments(b):
                dve.bn_stats(stats[:, b, 0, :], h0[:, b, 0:D // 2])
                link(dve.bn_stats(stats[:, b, 1, :], h0[:, b, D // 2:D]))
                link(dve.bn_aggr(mv[:, b, :], stats[:, b, :, :].rearrange("p a c -> p (a c)")))

            def norm(n, blocks=slice(0, NB), between=None):
                dve.tensor_scalar(std[:, blocks], mv[:, blocks, 1], EPS, None, ALU.add).then_inc(s_var, 1)
                if between:
                    between()
                dve.wait_ge(s_std, n + 1)
                link(dve.reciprocal(rstd[:, blocks], std[:, blocks]))
                dve.scalar_tensor_tensor(nmr[:, blocks], mv[:, blocks, 0], -1.0, rstd[:, blocks], ALU.mult,
                                         ALU.mult).then_inc(s_ln, 1)

            dve.memset(zeros[:, :], 0.0)
            dve.memset(zerof[:, :], 0.0)
            dve.memset(ones[:, :], 1.0)
            dve.memset(carry_row[:, :, :], -BIG)
            link(dve.memset(srcs[:, :], 0))
            dve.wait_ge(s_const, 5)
            dve.tensor_scalar(ident[:, :], diff[:, :], 0.0, None, ALU.is_equal)
            dve.tensor_scalar(identb[:, :], diff[:, :], 0.0, None, ALU.is_equal)
            dve.tensor_scalar(ltmask[:, :], diff[:, :], 0.0, None, ALU.is_lt)
            dve.tensor_scalar(shift_up[:, :], diff[:, :], float(H), None, ALU.is_equal)
            dve.tensor_scalar(shift_dn[:, :], diff[:, :], float(-H), None, ALU.is_equal)
            dve.tensor_copy(iota_h[:, :], iota_t[:, :])
            for m in (ci, pi):
                lo, hi, bl = (m[:, i, :] if m is ci else m[:, i:i + 1] for i in (1, 2, 3))
                a = m[:, 0, :] if m is ci else m[:, 0:1]
                dve.tensor_scalar(hi, a, 5, None, ALU.arith_shift_right)
                link(dve.tensor_scalar(lo, a, 31, None, ALU.bitwise_and))
                link(dve.tensor_scalar(bl, lo, 2, None, ALU.arith_shift_right))
            link(dve.tensor_copy(pf[:, :], pi[:, :]))
            lo_p, j_p, b_p = pf[:, 1:2], pf[:, 2:3], pf[:, 3:4]
            dve.tensor_scalar(Mhi, ci[:, 1, :], lo_p, None, ALU.is_equal)
            dve.tensor_scalar(Mgroup, ci[:, 2, :], j_p, None, ALU.is_equal)
            dve.tensor_scalar(Msame, ci[:, 3, :], b_p, None, ALU.is_equal)
            dve.tensor_scalar(bm5[:, :], iota_t[:, 0:NB], b_p, None, ALU.is_equal)
            link(dve.tensor_scalar(lm5[:, :], iota_t[:, 0:NB], b_p, None, ALU.is_lt))
            dve.scalar_tensor_tensor(Mj, ci[:, 2, :], j_p, Mhi, ALU.is_gt, ALU.mult)
            dve.scalar_tensor_tensor(Mless, ci[:, 1, :], lo_p, Msame, ALU.is_gt, ALU.mult).then_inc(s_ident, 1)

            dve.wait_ge(s_load, 32)
            dve.tensor_copy(rawf, raw).then_inc(s_rawf, 1)
            dve.wait_ge(s_cols, 1)
            dve.tensor_copy(scol[:, :], ps[0:TE, TU:2 * TU])
            dve.tensor_copy(dint[:, 0, :], ps[0:TE, 0:TU])
            link(dve.tensor_copy(dcol[:, :], ps[0:TE, 0:TU]))
            dve.tensor_scalar(dint[:, 1, :], dint[:, 0, :], 5, None, ALU.arith_shift_right)
            dve.tensor_scalar(dint[:, 2, :], dint[:, 0, :], 31, None, ALU.bitwise_and)
            link(dve.tensor_scalar(dcol1[:, :], dcol[:, :], 1.0, None, ALU.add))
            link(dve.tensor_copy(hif[:, :, :], dint[:, 1:3, :]))
            for o, part in ((OH, 0), (OL, 1)):
                dve.tensor_tensor(o, hif[:, part, :].unsqueeze(2).to_broadcast([TE, TU, LO]),
                                  iota_t[0:TE, 0:LO].unsqueeze(1).to_broadcast([TE, TU, LO]),
                                  ALU.is_equal).then_inc(s_oh, 1)

            def ranks(c):
                def rank_of(t, j):
                    if j % 2 == 0 and live(t, UE, TU):
                        dve.wait_ge(s_rank, t - UE + 2)
                    dve.scalar_tensor_tensor(eqj[:, j % UE, :], dst_row[c % 2][:, bass.ds((t - c * CTU) * TE, TE)],
                                             dcol[:, bass.ds(t, 1)], ltmask[0:TE, 0:TE], ALU.is_equal, ALU.mult,
                                             accum_out=rank[:, bass.ds(t, 1)]).then_inc(s_rank, 1)
                dve.wait_ge(s_drow[c % 2], (c // 2 + 1) * 16)
                if c == 0:
                    for j in range(UR):
                        rank_of(j, j)
                with dve.Fori(max(c * CTU, UR), (c + 1) * CTU - UR + 1, UR) as t:
                    for j in range(UR):
                        rank_of(t + j, j)
            ranks(0)

            dve.wait_ge(s_x, NB * 16)
            for b in range(NB):
                moments(b)
            norm(0)

            dve.wait_ge(s_cnt, 1)
            ct3, tab3 = (m.rearrange("p (l q) -> p l q", l=LO) for m in (CT, TAB))
            link(dve.tensor_copy(ct3, ps_cnt.rearrange("p (q l) -> p l q", l=LO)))
            Lt, Lx, Li = Lq[:, 0, :], Lq[:, 1, :], Lq[:, 2, :]
            link(dve.tensor_reduce(Lt, ct3, AX.X, ALU.add))
            dve.tensor_reduce(Tq[:, :], Lt, AX.X, ALU.add)
            link(dve.tensor_tensor_scan(Li, Lt, zerof[:, :], 0.0, ALU.add, ALU.add))
            dve.tensor_scalar(TM[:, :], bm5[:, :], Tq[:, 0:1], None, ALU.mult)
            dve.tensor_tensor(Lx, Li, Lt, ALU.subtract).then_inc(s_lq, 1)
            link(dve.tensor_tensor_scan(TAB, CT, zerof[:, 0:1].to_broadcast([P, LO * Q]), 0.0, ALU.add, ALU.add))
            link(dve.tensor_tensor(TAB, TAB, CT, ALU.subtract))
            dve.wait_ge(s_base, 1)
            link(dve.tensor_scalar(nti[:, 0, :], ps[:, LO:LO + NB], float(P - 1), None, ALU.add))
            link(dve.tensor_scalar(nti[:, 1, :], nti[:, 0, :], 7, None, ALU.arith_shift_right))
            link(dve.tensor_copy(nt[:, 0, :], nti[:, 1, :]))
            dve.tensor_tensor_scan(nt[:, 1, :], nt[:, 0, :], zerof[:, 0:NB], 0.0, ALU.add, ALU.add)
            link(dve.tensor_tensor(nt[:, 2, :], nt[:, 0, :], lm5[:, :], ALU.mult))
            link(dve.tensor_reduce(nt[:, 3, 0:1], nt[:, 2, :], AX.X, ALU.add))
            link(dve.tensor_scalar(start[:, :], nt[:, 3, 0:1], float(P), None, ALU.mult))
            link(dve.scalar_tensor_tensor(base2[:, :], ps[:, 0:LO], start[:, 0:1], Lx, ALU.add, ALU.subtract))
            link(dve.tensor_tensor(tab3, tab3, base2[:, :].unsqueeze(2).to_broadcast([P, LO, Q]), ALU.add))

            def set_diag(g):
                if g >= 2:
                    dve.wait_ge(s_look, g - 1)
                for q in range(QG):
                    last = dve.tensor_tensor(diag[g % 2][:, q, :].rearrange("p (j l) -> p j l", j=QJ),
                                             TAB[:, g * QG + q::Q].unsqueeze(1).to_broadcast([P, QJ, LO]),
                                             Mgroup.rearrange("p (j l) -> p j l", j=QJ), ALU.mult)
                last.then_inc(s_diag, 1)
            set_diag(0)
            set_diag(1)
            link(dve.tensor_scalar(blkf[:, 0, :], iota_t[0:1, :], nt[0:1, 1, 0:1], None, ALU.is_ge))
            for b in range(1, NB - 1):
                link(dve.scalar_tensor_tensor(blkf[:, b % 2, :], iota_t[0:1, :], nt[0:1, 1, b:b + 1],
                                              blkf[:, (b - 1) % 2, :], ALU.is_ge, ALU.add))
            link(dve.tensor_copy(blk[:, :], blkf[:, (NB - 2) % 2, :]))
            by_turn = blk[:, 0:T].rearrange("a (k j) -> a j k", j=UN)
            for j in range(1, UN):
                dve.tensor_scalar(by_turn[:, j], by_turn[:, j], 3 * j, None, ALU.logical_shift_left)
            link(dve.tensor_copy(packed[:, :], by_turn[:, 0]))
            for j in range(1, UN):
                link(dve.tensor_tensor(packed[:, :], packed[:, :], by_turn[:, j], ALU.bitwise_or))

            def select(g):
                w, tt = QG * QJ * LO, slice(g * QG * QJ, (g + 1) * QG * QJ)
                dve.wait_ge(s_look, g + 1)
                dve.tensor_tensor(sel, ps[0:TE, w * (g % 2):w * (g % 2 + 1)],
                                  OL[:, tt, :].rearrange("p t l -> p (t l)"), ALU.mult).then_inc(s_sel, 1)
                dve.wait_ge(s_sel, g + 1)
                link(dve.tensor_reduce(pos[:, tt], sel.rearrange("p (t l) -> p t l", l=LO), AX.X, ALU.add))

            ranks(1)
            select(0)
            set_diag(2)
            select(1)
            set_diag(3)
            ranks(2)
            select(2)
            set_diag(4)
            select(3)
            ranks(3)
            select(4)
            dve.wait_ge(s_rank, TU)
            link(dve.tensor_tensor(dint[:, 0, :], pos[:, :], rank[:, :], ALU.add))
            dve.tensor_scalar(dint[:, 1, :], dint[:, 0, :], P - 1, None, ALU.bitwise_and)
            link(dve.tensor_scalar(dint[:, 2, :], dint[:, 0, :], 7, None, ALU.arith_shift_right))
            link(dve.tensor_copy(hif[:, :, :], dint[:, 1:3, :]))

            def permute(t, j, k):
                if live(t, UP, TU):
                    dve.wait_ge(s_permd, t - UP + 1)
                dve.tensor_scalar(perm_l[j][0], iota_h[0:TE, 0:P], hif[:, 0, bass.ds(t, 1)], None, ALU.is_equal)
                dve.tensor_scalar(perm_r[j], iota_h[0:TE, 0:T], hif[:, 1, bass.ds(t, 1)], None,
                                  ALU.is_equal).then_inc(s_perm, 1)
            tiles(dve, permute, n=TU, un=UP, turns=TURNS)

            dve.wait_ge(s_permd, TU)
            dve.tensor_copy(srcs[:, 0:T], ps_perm[:, 0:T])
            dve.memset(vcol[:, T:TP], 0.0)
            link(dve.tensor_copy(vcol[:, 0:T], ps_perm[:, T:2 * T]))
            dve.tensor_scalar(dloc_i[:, 0, :], vcol[:, 0:T], -1.0, None, ALU.add)
            link(dve.tensor_scalar(dloc[:, :], vcol[:, 0:T], 0.0, -1000.0, ALU.is_equal, ALU.mult))
            link(dve.tensor_scalar(dloc_i[:, 1, :], dloc_i[:, 0, :], P - 1, None, ALU.bitwise_and))
            link(dve.tensor_tensor(dloc[:, :], dloc[:, :], dloc_i[:, 1, :], ALU.add))
            dve.tensor_scalar(BWD.rearrange("p (a c h) -> p c a h", c=CH, h=H),
                              vcol[:, :].rearrange("p (c a) -> p c a", c=CH).unsqueeze(3).to_broadcast([P, CH, TC, H]),
                              1.0, None, ALU.add).then_inc(s_sorted, 1)
            dve.wait_ge(s_dlt, 1)
            dve.tensor_copy(dlT[:, 0, :], ps[:, 0:P]).then_inc(s_dlte, 1)
            dve.tensor_copy(dlT[0:T - P, 1, :], ps[0:T - P, P:2 * P]).then_inc(s_dlte, 1)
            dve.wait_ge(s_vt, 1)
            link(dve.tensor_copy(LT, ps_lt))
            dve.tensor_tensor(reset_f[:, 1:L], LT[:, 1:L], LT[:, 0:L - 1], ALU.not_equal)
            dve.tensor_tensor(reset_b[:, 0:L - 1], LT[:, 1:L], LT[:, 0:L - 1], ALU.not_equal).then_inc(s_vs, 1)
            dve.wait_ge(s_vse, 1)
            dve.tensor_tensor(reset_f[:, 0:1], LT[:, 0:1], ps[:, 256:257], ALU.not_equal)
            link(dve.tensor_tensor(reset_b[:, L - 1:L], LT[:, L - 1:L], ps[:, 257:258], ALU.not_equal))
            dve.tensor_scalar(reset_f, reset_f, -BIG, None, ALU.mult)
            link(dve.tensor_scalar(reset_b, reset_b, -BIG, None, ALU.mult))
            dve.tensor_reduce(ends[:, 0:1], reset_f, AX.X, ALU.add)
            dve.tensor_reduce(ends[:, 1:2], reset_b, AX.X, ALU.add).then_inc(s_vs, 1)
            dve.wait_ge(s_vse, 2)
            for i in range(2):
                link(dve.tensor_copy(rows[:, i, :].rearrange("a (h c) -> a c h", h=H),
                                     ps[0:1, i * P:(i + 1) * P].rearrange("a (c h) -> a c h", h=H)))

            def set_out(c):
                w = T * P // PARTS
                dve.wait_ge(s_dlb[c], 16)
                dve.tensor_scalar(onehotT[:, c * w:(c + 1) * w], onehotT[:, c * w:(c + 1) * w],
                                  iota_p[:, 0:1], None, ALU.is_equal).then_inc(s_ohT, 1)
            dve.sem_inc(s_edges, 1)
            set_out(0)

            def scores(layer):
                own_heads = H - HA

                def keep(g, j0):
                    dve.wait_ge(s_mul, (g + 1) * UN)
                    dve.tensor_copy(logits[:, bass.ds(g * UN * H, UN * H)].rearrange("p (t h) -> p t h", h=H)[
                        :, :, 0:own_heads], head_sums[:, j0:j0 + UN, :]).then_inc(s_kept, 1)

                def step(s, i, m):
                    j, k = i % UN, m * TURNS + i // UN
                    dve.wait_ge(s_gs[j], (layer * (T // UN) + k + 1) * 16)
                    if live(s, 3):
                        dve.wait_ge(s_mul, layer * T + s - 2)
                        if layer == 0:
                            dve.wait_ge(s_reda, s - 2)
                    if layer:
                        dve.scalar_tensor_tensor(Y[j % 3], G[j][:, 0:D], 0.0, attn_row[:, :], ALU.max, ALU.mult,
                                                 accum_out=logits[:, bass.ds(s * H, 1)]).then_inc(s_mul, 1)
                        return
                    c = own_heads * HD
                    dve.scalar_tensor_tensor(Y[j % 3][:, c:D], G[j][:, c:D], 0.0, attn_row[:, c:D],
                                             ALU.max, ALU.mult).then_inc(s_yact, 1)
                    if j == 0 and live(s, UI):
                        dve.wait_ge(s_kept, k - TURNS + 1)
                    for h in range(own_heads):
                        w = slice(h * HD, (h + 1) * HD)
                        last = dve.scalar_tensor_tensor(Y[j % 3][:, w], G[j][:, w], 0.0, attn_row[:, w], ALU.max,
                                                        ALU.mult, accum_out=head_sums[:, i, h:h + 1])
                    last.then_inc(s_mul, 1)
                    if j == 1 and live(s, UN):
                        keep(k - 1, (i // UN - 1) % TURNS * UN)
                if layer == 0:
                    for s in range(UI):
                        step(s, s, 0)
                    for c in range(1, PARTS):
                        set_out(c)
                tiles(dve, step, un=UI, first=0 if layer else UI)
                if layer == 0:
                    keep(UK - 1, UI - UN)

            def softmax(layer):
                dve.wait_ge(s_u, (layer + 1) * T)
                dve.wait_ge(s_mul, (layer + 1) * T)
                if layer == 0:
                    dve.wait_ge(s_kept, UK)
                    dve.wait_ge(s_reda, T)
                dve.tensor_tensor(*(m.rearrange(f"p ({o} h) -> p c a h", c=CH, h=H) for m, o in
                                    ((BWD, "a c"), (logits, "c a"), (ulog, "c a"))), ALU.add).then_inc(s_lg, 1)
                dve.wait_ge(s_lt, layer + 1)
                dve.tensor_tensor_scan(FWD, reset_f, ps_lt, -BIG, ALU.add, ALU.max)
                dve.tensor_tensor_scan(BWD[:, ::-1], reset_b[:, ::-1], ps_lt[:, ::-1], -BIG, ALU.add,
                                       ALU.max).then_inc(s_en, 1)
                dve.wait_ge(s_er, layer + 1)
                for i in range(2):
                    link(dve.tensor_copy(rows[:, 2 + i, :].rearrange("a (h c) -> a c h", h=H),
                                         ps[0:1, i * P:(i + 1) * P].rearrange("a (c h) -> a c h", h=H)))
                dve.tensor_tensor_scan(carry_row[:, 0, 1:P + 1], rows[:, 0, :], rows[:, 2, :], -BIG, ALU.add, ALU.max)
                link(dve.tensor_tensor_scan(carry_row[:, 1, 0:P][:, ::-1], rows[:, 1, ::-1], rows[:, 3, ::-1], -BIG,
                                            ALU.add, ALU.max))
                for i in range(2):
                    last = dve.tensor_copy(rows[:, 2 + i, :].rearrange("a (c h) -> a c h", h=H),
                                           carry_row[:, i, i:i + P].rearrange("a (h c) -> a c h", h=H))
                last.then_inc(s_cr, 1)
                dve.wait_ge(s_ca, layer + 1)
                link(dve.tensor_copy(carry[:, :], ps[:, 256:258]))
                dve.tensor_tensor_scan(FWD, reset_f, ps_lt, carry[:, 0:1], ALU.add, ALU.max)
                link(dve.tensor_tensor_scan(BWD[:, ::-1], reset_b[:, ::-1], ps_lt[:, ::-1], carry[:, 1:2], ALU.add,
                                            ALU.max))
                link(dve.tensor_tensor(FWD, FWD, BWD, ALU.max))
                dve.tensor_tensor(LT, ps_lt, FWD, ALU.subtract).then_inc(s_m, 1)
                dve.wait_ge(s_et, layer + 1)
                dve.tensor_copy(logits.rearrange("p (c a h) -> p a c h", c=CH, h=H),
                                ps_lt.rearrange("p (a c h) -> p a c h", c=CH, h=H)).then_inc(s_exd, 1)
                dve.wait_ge(s_exd, layer + 1)

            def aggregate(layer):
                if layer:
                    ex = logits[:, 0:T * H].rearrange("p (t h) -> p t h", h=H)[:, :, 0]
                    dve.wait_ge(s_z, 2 * T)
                    dve.tensor_copy(src_col, srcs[:, 0:T])
                    link(dve.tensor_copy(ex_cast, ex))
                    link(dve.tensor_copy(ex_part[:, 0, :], ex_cast))
                    link(dve.tensor_tensor(ex_part[:, 2, :], ex, ex_part[:, 0, :], ALU.subtract))
                    link(dve.tensor_copy(ex_cast, ex_part[:, 2, :]))
                    link(dve.tensor_copy(ex_part[:, 1, :], ex_cast))
                    dve.tensor_tensor(ex_part[:, 2, :], ex_part[:, 2, :], ex_part[:, 1, :],
                                      ALU.subtract).then_inc(s_part, 1)
                    dve.wait_ge(s_col, 1)

                def step(s, j, k):
                    if live(s, 3):
                        dve.wait_ge(s_agg, layer * T + s - 2)
                    if layer == 0:
                        dve.tensor_scalar(oh_agg[j % 3], iota_t[:, 0:P], dloc[:, bass.ds(s, 1)], None,
                                          ALU.is_equal).then_inc(s_oha, 1)
                        dve.wait_ge(s_ga[j], (k + 1) * 16)
                        dve.tensor_tensor(WG[j % 3][:, 0:D].rearrange("p (h d) -> p h d", h=H),
                                          G[j][:, 0:D].rearrange("p (h d) -> p h d", h=H),
                                          logits[:, bass.ds(s * H, H)].unsqueeze(2).to_broadcast([P, H, HD]),
                                          ALU.mult).then_inc(s_wg, 1)
                    else:
                        dve.tensor_scalar(oh_dst[j % 3], iota_h[:, 0:P], dloc[:, bass.ds(s, 1)], None,
                                          ALU.is_equal).then_inc(s_ohd, 1)
                        dve.tensor_scalar(oh_ex[j % 3][:, 0, :], iota_h[:, 0:P], dloc[:, bass.ds(s, 1)],
                                          ex_part[:, 0, bass.ds(s, 1)], ALU.is_equal, ALU.mult)
                        dve.tensor_scalar(oh_src[j % 3], iota_s, src_col[:, bass.ds(s, 1)], None,
                                          ALU.is_equal).then_inc(s_ohs, 1)
                tiles(dve, step, turns=TURNS)

            def finish(layer):
                if layer == 0:
                    dve.wait_ge(s_agg, T)
                    c0, c1, at, step = PIECES[-1]
                    dens = ps[:, at:at + NB * step].rearrange("p (b c) -> p b c", b=NB)[:, :, D - c0:FW - c0]
                    link(dve.tensor_scalar(rden[:, :, :], dens, 1e-30, None, ALU.max))
                else:
                    dve.wait_ge(s_dense, NB)
                    link(dve.tensor_reduce(rden[:, :, 1], row_sum[:, :, :], AX.X, ALU.add))
                    link(dve.tensor_scalar(rden[:, :, 0], rden[:, :, 1], 1e-30, None, ALU.max))
                heads = 1 if layer else H
                dve.reciprocal(rden[:, :, 0:heads], rden[:, :, 0:heads]).then_inc(s_rden, 1)

                def elu(b):
                    if layer == 0:
                        dve.wait_ge(s_exp, b + 1)
                        dve.wait_ge(s_radd, b + 1)
                        v = h0[:, b, :]
                    else:
                        dve.wait_ge(s_sum, NB + b + 1)
                        v = agg_v[b]
                        link(dve.tensor_scalar(v, v, -1.0, None, ALU.add))
                    dve.scalar_tensor_tensor(h0[:, b, :], agg_e[b % 3], 1.0, v, ALU.min, ALU.add).then_inc(s_elu, 1)
                    dve.wait_ge(s_elu, layer * NB + b + 1)
                    moments(b)

                def affine(b):
                    dve.wait_ge(s_nrm, layer * NB + b + 1)
                    link(dve.tensor_tensor(h0[:, b, :], h0[:, b, :], lnw_row, ALU.mult))
                    if layer == 0:
                        dve.tensor_tensor(h0[:, b, :], h0[:, b, :], lnb_row, ALU.add).then_inc(s_h, 1)
                    else:
                        n = min(P, N - b * P)
                        dve.wait_ge(s_xb, b + 1)
                        dve.tensor_tensor(h0[0:n, b, :], h0[0:n, b, :], Wm[0:n, b, :], ALU.add).then_inc(s_res, 1)

                if layer == 0:
                    for i in range(NB + 2):
                        if i < NB:
                            v = agg_v[i].rearrange("p (h d) -> p h d", h=H)
                            dve.wait_ge(s_sum, i + 1)
                            dve.tensor_tensor(v, v, rden[:, i, :].unsqueeze(2).to_broadcast([P, H, HD]),
                                              ALU.mult).then_inc(s_div, 1)
                        if i >= 2:
                            elu(i - 2)
                    norm(1)
                    dve.wait_ge(s_lnr, 32)
                    for b in range(NB):
                        affine(b)
                else:
                    for b in range(NB - 1):
                        elu(b)
                    norm(2, slice(0, NB - 1))
                    dve.wait_ge(s_lnr, 64)
                    for b in range(NB - 2):
                        affine(b)
                    elu(NB - 1)
                    norm(3, slice(NB - 1, NB), lambda: affine(NB - 2))
                    affine(NB - 1)

            for layer in range(2):
                if layer:
                    dve.wait_ge(s_rows, 96)
                    dve.wait_ge(s_attn, 2)
                    for u in range(2 * NB):
                        n, f = 2 * NB + u, ftile[u % 2]
                        dve.wait_ge(s_pe, len(PROJ) + PROJ.index(("DF"[u // NB], u % NB)) + 1)
                        dve.tensor_tensor(f[:, 0:D], f[:, 0:D], bias[u // NB][:, :], ALU.add).then_inc(s_fb, 1)
                        dve.wait_ge(s_fb, n + 1)
                        dve.wait_ge(s_um, n)
                        dve.scalar_tensor_tensor(utmp[:, :], f[:, 0:D], SLOPE / (1.0 - SLOPE), attn_row[:, :],
                                                 ALU.mult, ALU.mult, accum_out=f[:, D:D + 1]).then_inc(s_um, 1)
                dve.wait_ge(s_pp, (layer + 1) * len(PROJ))
                if layer == 0:
                    dve.memset(logits[:, T * H:TP * H], 0.0)
                    dve.memset(ulog[:, T * H:TP * H], 0.0).then_inc(s_clear, 1)
                else:
                    dve.memset(R3[:, 0:2 * TP * H], 0.0).then_inc(s_clear, 1)
                dve.wait_ge(s_clear, layer + 1)
                scores(layer)
                softmax(layer)
                aggregate(layer)
                finish(layer)

        @block.tensor
        def _(pe):
            pe.wait_ge(s_ident, 1)
            pe.wait_ge(s_rawf, 1)
            for v in range(4):
                last = pe.transpose(ps[0:TE, v * 80:(v + 1) * 80], rawf[:, v, :], ident[0:80, 0:80])
            last.then_inc(s_cols, 1)
            pe.wait_ge(s_oh, 2)
            for t in range(TU):
                q, j = t // QJ, t % QJ
                last = pe.matmul(ps_cnt[32 * j:32 * j + 32, q * LO:(q + 1) * LO], OH[:, t, :], OL[:, t, :],
                                 start=True, stop=True)
            last.then_inc(s_cnt, 1)
            for g in range(Q // 8):
                if g:
                    pe.wait_ge(s_ohte, g)
                for q in range(8):
                    t = (g * 8 + q) * QJ
                    last = pe.transpose(ps_ohT[:, q, 0:TE], OH[:, t:t + QJ, :].rearrange("p t l -> p (t l)"),
                                        identb[0:TE, 0:TE])
                last.then_inc(s_oht, 1)

            def offsets():
                pe.wait_ge(s_ohte, Q // 8)
                pe.wait_ge(s_lq, 1)
                pe.matmul(ps[:, 0:LO], Mhi, Lq[:, 1, :], start=True, stop=False)
                pe.matmul(ps[:, 0:LO], Mj, Lq[:, 0, :], start=False, stop=False)
                pe.matmul(ps[:, 0:LO], Mless, Tq[:, 0:1].to_broadcast([P, LO]), start=False, stop=True)
                pe.matmul(ps[:, LO:LO + NB], ones[:, :], TM[:, :], start=True, stop=True).then_inc(s_base, 1)

            def look_up(g):
                pe.wait_ge(s_diag, g + 1)
                if g >= 2:
                    pe.wait_ge(s_sel, g - 1)
                for q in range(QG):
                    at = (g % 2 * QG + q) * P
                    last = pe.matmul(ps[0:TE, at:at + P], OHT[:, g * QG + q, :], diag[g % 2][:, q, :],
                                     start=True, stop=True)
                last.then_inc(s_look, 1)

            def project(layer, first=0, end=len(PROJ)):
                for i, (kind, b) in list(enumerate(PROJ))[first:end]:
                    if layer == 0 and (kind, b) in PART:
                        permute(PART[kind, b])
                    n = layer * len(PROJ) + i
                    if n >= 2:
                        pe.wait_ge(s_pe, n - 1)
                    o = slot[i % 2]
                    if kind == "T":
                        pe.wait_ge(s_h, layer * NB + b + 1)
                        for k in range(KC):
                            last = pe.transpose(o[:, k * P:(k + 1) * P], h0[:, b, k * P:(k + 1) * P], ident[:, :])
                    else:
                        pe.wait_ge(s_pe, layer * len(PROJ) + PROJ.index(("T", b)) + 1)
                        v = 2 * layer + (kind == "F")
                        for k in range(KC):
                            pe.wait_ge(s_wk[k], (v + 1) * 16)
                            for c0, c1 in ((0, 512), (512, D)):
                                last = pe.matmul(o[:, c0:c1], hT[:, k, b * P:(b + 1) * P],
                                                 (Wn if v == 3 else Wm)[:, k, c0:c1],
                                                 start=k == 0, stop=k == KC - 1)
                            if v == 0 and b == NB - 1 and k < KC - 1:
                                last.then_inc(s_wu, 1)
                    last.then_inc(s_pp, 1)
                    if layer == 0 and (kind, b) == ("D", NB - 1):
                        pe.wait_ge(s_pp, n + 1)
                        pe.sem_inc(s_wu, 1)

            turn = [None]

            def block_of(j, k):
                if j == 0:
                    turn[0] = pe.value_load(packed[0:1, bass.ds(k, 1)])
                b = turn[0] // 8 ** j % 8
                return nc.s_assert_within(b, 0, NB - 1, skip_runtime_bounds_check_because="it counts the block ends, "
                                          "of which there are NB - 1 before the last, that a tile lies beyond")

            def scores(layer):
                def step(s, j, k):
                    b = block_of(j, k)
                    if live(s, 3):
                        pe.wait_ge(s_zc, layer * T + s - 2)
                    for part in range(3):
                        for c0, c1 in ((0, 512), (512, FW)):
                            last = pe.matmul(psz[j % 3][:, c0:c1], onehotT[:, bass.ds(s * P, P)],
                                             FD[part][:, bass.ds(b * FW + c0, c1 - c0)],
                                             start=part == 0, stop=part == 2)
                    last.then_inc(s_z, 1)
                for c in range(PARTS):
                    pe.wait_ge(s_ohT, c + 1)
                    tiles(pe, step, n=(c + 1) * T // PARTS, first=c * T // PARTS, turns=TURNS)

            def softmax(layer):
                pe.wait_ge(s_lg, layer + 1)
                for a in range(TC):
                    last = pe.transpose(ps_lt[:, a * P:(a + 1) * P], BWD[:, a * P:(a + 1) * P], ident[:, :])
                last.then_inc(s_lt, 1)
                pe.wait_ge(s_en, layer + 1)
                pe.transpose(ps[0:1, 0:P], FWD[:, L - 1:L], ident[:, :])
                pe.transpose(ps[0:1, P:2 * P], BWD[:, 0:1], ident[:, :]).then_inc(s_er, 1)
                pe.wait_ge(s_cr, layer + 1)
                pe.transpose(ps[:, 256:257], rows[:, 2, :], ident[0:1, 0:1])
                pe.transpose(ps[:, 257:258], rows[:, 3, :], ident[0:1, 0:1]).then_inc(s_ca, 1)
                pe.wait_ge(s_ex, layer + 1)
                for a in range(TC):
                    last = pe.transpose(ps_lt[:, a * P:(a + 1) * P], LT[:, a * P:(a + 1) * P], ident[:, :])
                last.then_inc(s_et, 1)

            def aggregate(layer):
                pe.wait_ge(s_exd, layer + 1)
                for b in range(8):
                    pe.matmul(ps[:, b * 512:(b + 1) * 512], zeros[:, 0:P], zeros[:, :], start=True, stop=True,
                              skip_group_check=True)

                def step(s, j, k):
                    b = block_of(j, k)
                    if layer == 0:
                        pe.wait_ge(s_oha, s + 1)
                        pe.wait_ge(s_wg, s + 1)
                        pe.wait_ge(s_wd, s + 1)
                        for c0, c1, at, step in PIECES:
                            last = pe.matmul(ps[:, bass.ds(b * step + at, c1 - c0)], oh_agg[j % 3],
                                             WG[j % 3][:, c0:c1], start=False, stop=False, skip_group_check=True)
                    else:
                        pe.wait_ge(s_ohs, s + 1)
                        pe.wait_ge(s_ohx1, s + 1)
                        pe.wait_ge(s_ohx2, s + 1)
                        for c0, c1, at, step in SPAN:
                            for v in range(3):
                                last = pe.matmul(ps[:, bass.ds(b * step + at, c1 - c0)], oh_ex[j % 3][:, v, :],
                                                 oh_src[j % 3][:, c0:c1], start=False, stop=False,
                                                 skip_group_check=True)
                    last.then_inc(s_agg, 1)
                tiles(pe, step, turns=TURNS)
                if layer == 0:
                    return
                pe.wait_ge(s_dense, NB)
                for i in range(NB * NB):
                    last = pe.transpose(ps[:, i * P:(i + 1) * P], dense[:, i // NB, i % NB * P:(i % NB + 1) * P],
                                        ident[:, :])
                    if i % 4 == 3 or i == NB * NB - 1:
                        last.then_inc(s_tr, 1)
                pe.wait_ge(s_tre, -(-NB * NB // 4))
                pe.wait_ge(s_fs, NB * 16)
                for b in range(NB):
                    if b >= 4:
                        pe.wait_ge(s_sum, NB + b - 3)
                    for c0, c1 in ((0, 512), (512, D)):
                        for c in range(NB):
                            last = pe.matmul(prod[b % 4][:, c0:c1], denseT[:, b * NB + c, :], FS[:, c, c0:c1],
                                             start=c == 0, stop=c == NB - 1)
                    last.then_inc(s_prod, 1)

            def permute(c):
                if c == 0:
                    pe.wait_ge(s_sel, Q // QG)
                    pe.matmul(ps[:, 512:1024], zeros[:, 0:P], zeros[:, :], start=True, stop=True,
                              skip_group_check=True)

                def step(t, j, k):
                    pe.wait_ge(s_scaled0, t + 1)
                    pe.wait_ge(s_scaled1, t + 1)
                    for v in range(2):
                        last = pe.matmul(ps_perm[:, v * T:(v + 1) * T], perm_l[j][1 + v], perm_r[j], start=False,
                                         stop=False, skip_group_check=True)
                    last.then_inc(s_permd, 1)
                tiles(pe, step, n=(c + 1) * PT, un=UP, first=c * PT, turns=TURNS)

            project(0, 0, 2)
            offsets()
            project(0, 2, 5)
            look_up(0)
            look_up(1)
            project(0, 5, 7)
            look_up(2)
            look_up(3)
            project(0, 7, 9)
            look_up(4)
            project(0, 9)
            pe.wait_ge(s_sorted, 1)
            pe.transpose(ps[:, 0:P], dloc[:, 0:P], ident[:, :])
            pe.transpose(ps[0:T - P, P:2 * P], dloc[:, P:T], ident[:, :]).then_inc(s_dlt, 1)
            for a in range(TC):
                last = pe.transpose(ps_lt[:, a * P:(a + 1) * P], BWD[:, a * P:(a + 1) * P], ident[:, :])
            last.then_inc(s_vt, 1)
            pe.wait_ge(s_vs, 1)
            pe.matmul(ps[:, 256:257], shift_up[:, :], LT[:, L - 1:L], start=True, stop=True)
            pe.matmul(ps[:, 257:258], shift_dn[:, :], LT[:, 0:1], start=True, stop=True).then_inc(s_vse, 1)
            pe.wait_ge(s_dlte, 2)
            pe.wait_ge(s_vs, 2)
            pe.transpose(ps[0:1, 0:P], ends[:, 0:1], ident[:, :])
            pe.transpose(ps[0:1, P:2 * P], ends[:, 1:2], ident[:, :]).then_inc(s_vse, 1)
            for layer in range(2):
                if layer:
                    project(1)
                pe.wait_ge(s_fd, (layer + 1) * NB)
                pe.wait_ge(s_pe, (layer + 1) * len(PROJ))
                scores(layer)
                softmax(layer)
                aggregate(layer)


INS = ["x", "src", "dst", "L0_gnn_W1s", "L0_gnn_b1s", "L0_gnn_W1d", "L0_gnn_b1d", "L0_gnn_attn1",
       "L0_gnn_ln1_w", "L0_gnn_ln1_b", "L0_gnn_Wos", "L0_gnn_bos", "L0_gnn_Wod", "L0_gnn_bod",
       "L0_gnn_attno", "L0_gnn_lno_w", "L0_gnn_lno_b"]


def kernel(**inputs):
    import numpy as np
    import concourse.bacc as bacc
    from concourse.bass_utils import run_bass_kernel_spmd

    nc = bacc.Bacc("TRN2", target_bir_lowering=False, num_devices=1)
    arrays, args = {}, []
    for name in INS:
        a = np.ascontiguousarray(inputs[name])
        arrays[f"in_{name}"] = a
        args.append(nc.dram_tensor(f"in_{name}", a.shape, mybir.dt.from_np(a.dtype), kind="ExternalInput").ap())
    args.append(nc.dram_tensor("out_0", (N, D), f32, kind="ExternalOutput").ap())
    gnn_program(nc, *args)
    r = run_bass_kernel_spmd(nc, [arrays], core_ids=[0])
    return r.results[0]["out_0"]
```
